# Optimizing a Trainium2 kernel written in Bass

```python
import numpy as np
import jax
import jax.numpy as jnp

def _softmax(x, axis=-1):
    return jax.nn.softmax(x, axis=axis)

def _gelu(x):
    return jax.nn.gelu(x, approximate=True)

def _silu(x):
    return jax.nn.silu(x)

def _sigmoid(x):
    return jax.nn.sigmoid(x)

def _layernorm(x, axis=-1, eps=1e-05):
    m = jnp.mean(x, axis=axis, keepdims=True)
    v = jnp.var(x, axis=axis, keepdims=True)
    return (x - m) / jnp.sqrt(v + eps)

def _scatter_add(tgt, idx, src, axis=0):
    return tgt.at[idx].add(src)

def _segment_sum(src, seg, n):
    return jax.ops.segment_sum(src, seg, n)
kernel_name = 'mk_macaron_d1_jaxref_r4_12f82f'

def setup_inputs(seed: int=0):
    np.random.seed(seed)
    _w = jnp.asarray

    def _L0_attn_setup():
        import jax, jax.numpy as jnp
        import numpy as np
        import math
        B, T, E, H = (4, 512, 256, 16)
        D = E // H
        rng = jax.random.key(seed)
        k1, k2, k3, k4, k5 = jax.random.split(rng, 5)
        scale_w = 1.0 / math.sqrt(E)
        return {'query': jax.random.normal(k1, (B, T, E), jnp.float32), 'key': jax.random.normal(k2, (B, T, E), jnp.float32), 'value': jax.random.normal(k3, (B, T, E), jnp.float32), 'in_proj_weight': jax.random.normal(k4, (3 * E, E), jnp.float32) * scale_w, 'out_proj_weight': jax.random.normal(k5, (E, E), jnp.float32) * scale_w}
    _L0_attn_in = _L0_attn_setup()

    def _L0_ffn_setup():
        import jax, jax.numpy as jnp
        import numpy as np
        E = 8
        K = 2
        D = 256
        B, N = (4, 1024)
        DC = 128
        key = jax.random.key(seed)
        ks = jax.random.split(key, 6)
        x = jax.random.normal(ks[0], (B, N, D), jnp.float32)
        cond = jax.random.normal(ks[1], (B, N, DC), jnp.float32)
        mask = jnp.ones((B, N), jnp.float32)
        W_shared = jax.random.normal(ks[2], (D, D), jnp.float32) * 0.02
        W_expert = jax.random.normal(ks[3], (D, D), jnp.float32) * 0.02
        W_gate = jax.random.normal(ks[4], (D, E - 1), jnp.float32) * 0.02
        bias = jnp.zeros((D,), jnp.float32)
        return dict(x=x, cond=cond, mask=mask, W_shared=W_shared, W_expert=W_expert, W_gate=W_gate, bias=bias)
    _L0_ffn_in = _L0_ffn_setup()
    _d = {'L0_attn_query': _L0_attn_in['query'], 'L0_attn_key': _L0_attn_in['key'], 'L0_attn_value': _L0_attn_in['value'], 'L0_attn_in_proj_weight': _L0_attn_in['in_proj_weight'], 'L0_attn_out_proj_weight': _L0_attn_in['out_proj_weight'], 'L0_ffn_cond': _L0_ffn_in['cond'], 'L0_ffn_mask': _L0_ffn_in['mask'], 'L0_ffn_W_shared': _L0_ffn_in['W_shared'], 'L0_ffn_W_expert': _L0_ffn_in['W_expert'], 'L0_ffn_W_gate': _L0_ffn_in['W_gate'], 'L0_ffn_bias': _L0_ffn_in['bias']}
    _x0 = _d['L0_attn_query']
    _d['L0_attn_query'] = jax.random.normal(jax.random.fold_in(jax.random.key(seed), 1), (8, 1024, 256), dtype=_x0.dtype)
    del _x0
    return _d

def reference(L0_attn_query, L0_attn_key, L0_attn_value, L0_attn_in_proj_weight, L0_attn_out_proj_weight, L0_ffn_cond, L0_ffn_mask, L0_ffn_W_shared, L0_ffn_W_expert, L0_ffn_W_gate, L0_ffn_bias):

    def _L0_attn_ref(query, key, value, in_proj_weight, out_proj_weight):
        import jax, jax.numpy as jnp
        import numpy as np
        import math
        B, T, E, H = (4, 512, 256, 16)
        D = E // H
        b, t, e = query.shape
        qkv = jnp.einsum('bte,fe->btf', query, in_proj_weight).reshape(b, t, 3, H, D)
        q = jnp.transpose(qkv[:, :, 0], (0, 2, 1, 3))
        k = jnp.transpose(qkv[:, :, 1], (0, 2, 1, 3))
        v = jnp.transpose(qkv[:, :, 2], (0, 2, 1, 3))
        q = q / math.sqrt(D)
        scores = jnp.einsum('bhqd,bhkd->bhqk', q, k)
        pos = jnp.arange(t)
        causal = pos[:, None] >= pos[None, :]
        scores = jnp.where(causal[None, None], scores, jnp.float32(-jnp.inf))
        attn = jax.nn.softmax(scores, axis=-1)
        out = jnp.einsum('bhqk,bhkd->bhqd', attn, v)
        out = jnp.transpose(out, (0, 2, 1, 3)).reshape(b, t, e)
        out = jnp.einsum('bte,fe->btf', out, out_proj_weight)
        return out

    def _L0_ffn_ref(x, cond, mask, W_shared, W_expert, W_gate, bias):
        import jax, jax.numpy as jnp
        import numpy as np
        E = 8
        K = 2
        D = 256
        B, N = (4, 1024)
        DC = 128
        b, n, d = x.shape
        T = b * n
        xf = x.reshape(T, d)
        scores = jax.nn.softmax(xf @ W_gate, axis=-1)
        expert_weights, _ = jax.lax.top_k(scores, K)
        expert_weights = expert_weights / expert_weights.sum(-1, keepdims=True)
        expert_indices = (jnp.arange(T * K) % E).reshape(T, K)
        te = expert_indices.reshape(-1)
        w = expert_weights.reshape(-1)
        capacity = K * T // E
        order = jnp.argsort(te, stable=True)
        sorted_e = te[order]
        hist = jnp.bincount(te, length=E)
        starts = jnp.concatenate([jnp.zeros((1,), hist.dtype), jnp.cumsum(hist)[:-1]])
        pos = jnp.arange(T * K) - starts[sorted_e]
        valid = pos < capacity
        dest = jnp.where(valid, sorted_e * capacity + pos, E * capacity)
        tok = order // K
        gathered = jnp.zeros((E * capacity + 1, d), x.dtype).at[dest].set(xf[tok])
        gathered = gathered[:-1]
        y = gathered @ W_expert.T
        contrib = w[order][:, None] * y[jnp.minimum(dest, E * capacity - 1)]
        moe_out = jnp.zeros((T, d), x.dtype).at[tok].add(jnp.where(valid[:, None], contrib, 0.0))
        shared = xf @ W_shared.T
        out = (shared + moe_out + bias).reshape(b, n, d)
        return out
    x = L0_attn_query
    x = x + 0.5 * _L0_ffn_ref(_layernorm(x, axis=-1), L0_ffn_cond, L0_ffn_mask, L0_ffn_W_shared, L0_ffn_W_expert, L0_ffn_W_gate, L0_ffn_bias)
    x = x + _L0_attn_ref(_layernorm(x, axis=-1), L0_attn_key, L0_attn_value, L0_attn_in_proj_weight, L0_attn_out_proj_weight)
    x = x + 0.5 * _L0_ffn_ref(_layernorm(x, axis=-1), L0_ffn_cond, L0_ffn_mask, L0_ffn_W_shared, L0_ffn_W_expert, L0_ffn_W_gate, L0_ffn_bias)
    return x

_drawn_inputs = setup_inputs


def setup_inputs(seed=0):
    import zlib

    import numpy as np

    out = dict(_drawn_inputs(seed))
    spreads = {'L0_ffn_bias': (0.0, 0.1)}
    factors = {}
    for name, (base, spread) in spreads.items():
        noise = np.random.default_rng([zlib.crc32(name.encode()), seed]).standard_normal(out[name].shape)
        drawn = base * np.exp(spread * noise) if base else spread * noise
        out[name] = jnp.asarray(drawn.astype(out[name].dtype))
    for name, factor in factors.items():
        out[name] = (out[name] * factor).astype(out[name].dtype)
    return out
```

```python
from contextlib import ExitStack

import concourse.bass as bass
from concourse import mybir

F32 = mybir.dt.float32
F32R = mybir.dt.float32r
BF16 = mybir.dt.bfloat16
ALU = mybir.AluOpType
ACT = mybir.ActivationFunctionType
AX = mybir.AxisListType

P = 128
B, T, E = 8, 1024, 256
H, D = 16, 16
NEXP = 7
EPS = 1e-5
CHUNK = 512
TPC = CHUNK // P
NCHUNK = B * T // CHUNK
KC = E // P
GH = 4
NG = B * H // GH
GPB = H // GH
KT = T // P
BANK = 512
YL = E + NEXP + 1

W_QK, W_V, W_SH, W_EX, W_OUT = 0, 2 * E, 3 * E, 4 * E, 4 * E + YL
WCOLS = W_OUT + E

SROWS = 4 * D
SROWS_M = SROWS + 2
NBUF = 3
AHEAD = 3
MASKED = -1.0e38

SLOTS = [
    [(0, 0, 512, 0)],
    [(0, 512, 512, 0)],
    [(1, 128, 384, 0), (7, 896, 128, 384)],
    [(2, 256, 256, 0), (6, 768, 256, 256)],
    [(3, 384, 128, 0), (5, 640, 384, 128)],
    [(1, 512, 512, 0)],
    [(2, 512, 512, 0)],
    [(3, 512, 512, 0)],
    [(4, 512, 512, 0)],
]
NSLOT = len(SLOTS)
TILES = NSLOT * GH
DIAG = [[off for j, q0, n, off in s if q0 == j * P] for s in SLOTS]
DIAG_SLOTS = [s for s in range(NSLOT) if DIAG[s]]
LOW_DONE, HIGH_DONE = 4, 8

MAX_SLOTS = [
    [(3, 0, 512, 0)],
    [(7, 512, 512, 0)],
    [(7, 0, 512, 0)],
    [(6, 0, 512, 0)],
    [(5, 0, 512, 0)],
    [(4, 0, 512, 0)],
    [(2, 0, 384, 0), (0, 0, 128, 384)],
    [(6, 512, 384, 0), (4, 512, 128, 384)],
    [(1, 0, 256, 0), (5, 512, 256, 256)],
]
SB = 3
M_BANK = 1


class Arena:

    def __init__(self, nc, ctx, hold=None):
        self.nc, self.ctx, self.hold = nc, ctx, hold

    def sb(self, name, shape, dt=F32):
        return self.ctx.enter_context(self.nc.sbuf_tensor(name, shape, dt))

    def sem(self, name):
        return self.ctx.enter_context(self.nc.semaphore(name))


class Chain:

    def __init__(self, eng, sem, base):
        self.eng, self.sem, self.base, self.n = eng, sem, base, 0

    def __call__(self, ins):
        ins.then_inc(self.sem, 1)
        self.n += 1
        self.eng.wait_ge(self.sem, self.base + self.n)


class Hold:

    COLS = 8

    def __init__(self, ar):
        self.dve_out = ar.sb("hold_dve", [P, self.COLS])
        self.pool_out = ar.sb("hold_pool", [P, self.COLS])

    def dve(self, dve, col):
        dve.memset(self.dve_out[:, col:col + 1], 0.0)

    def pool(self, pool, col, zero):
        pool.tensor_tensor(self.pool_out[:, col:col + 1], zero[:, 0:1], zero[:, 1:2], ALU.add)


def project(pe, out, lh, ll, rh, rl):
    terms = [(a[ch], b[ch]) for ch in range(KC) for a, b in ((lh, rh), (lh, rl), (ll, rh))]
    for n, (a, b) in enumerate(terms):
        last = pe.matmul(out, a, b, start=(n == 0), stop=(n == len(terms) - 1))
    return last


GATE_LINKS = 10


class Ffn:

    def __init__(self, ar, name, w, banks, zero, col=0):
        self.w, self.banks, self.hold = w, banks, ar.hold
        sb, sem = (lambda n, s, d=F32: ar.sb(f"{name}_{n}", s, d)), (lambda n: ar.sem(f"{name}_{n}"))
        self.stats = sb("stats", [P, TPC, 6])
        self.mv = sb("mv", [P, TPC, 2])
        self.veps = sb("veps", [P, TPC])
        self.nmean = sb("nmean", [P, TPC])
        self.zero, self.col = zero, col
        self.rstd = sb("rstd", [P, TPC])
        self.nbias = sb("nbias", [P, TPC])
        self.xn = sb("xn", [P, TPC, E])
        self.xh = sb("xh", [P, KC, CHUNK], F32R)
        self.xl = sb("xl", [P, KC, CHUNK], F32R)
        self.bn_done = sem("bn_done")
        self.mv_ready = sem("mv_ready")
        self.pool_chain = sem("pool_chain")
        self.xn_ready = sem("xn_ready")
        self.t_ready = sem("t_ready")
        self.xh_ready = sem("xh_ready")
        self.xl_ready = sem("xl_ready")

    def dve_stats(self, dve, k, t, x):
        dve.bn_stats(self.stats[:, t, :], x[:, t, :]).then_inc(self.bn_done, 1)

    def dve_aggregate(self, dve, k, first=False):
        dve.wait_ge(self.bn_done, k * TPC + TPC)
        if not first:
            dve.wait_ge(self.xn_ready, k * TPC)
        self.hold.dve(dve, self.col)
        for t in range(TPC):
            dve.bn_aggr(self.mv[:, t, :], self.stats[:, t, :]).then_inc(self.mv_ready, 1)

    def pool_rstd(self, pool, k, mhalf, first=False):
        ch = Chain(pool, self.pool_chain, k * 4)
        pool.wait_ge(self.mv_ready, k * TPC + TPC)
        if not first:
            pool.wait_ge(self.xn_ready, k * TPC)
        pool.tensor_tensor(self.nmean[:], self.zero[:], self.mv[:, :, 0], ALU.subtract).then_inc(self.pool_chain, 1)
        ch.n += 1
        ch(pool.tensor_scalar(self.veps[:], self.mv[:, :, 1], EPS, None, ALU.add))
        ch(pool.tensor_tensor(self.rstd[:], self.veps[:], mhalf[:], ALU.pow))
        pool.tensor_tensor(self.nbias[:], self.nmean[:], self.rstd[:], ALU.mult).then_inc(self.pool_chain, 1)

    def act_normalise(self, act, k, x, first=False, tiles=range(TPC)):
        if tiles[0] == 0:
            act.wait_ge(self.pool_chain, k * 4 + 4)
            if not first:
                act.wait_ge(self.t_ready, k * KC)
        for t in tiles:
            act.activation(self.xn[:, t, :], x[:, t, :], ACT.Identity, scale=self.rstd[:, t:t + 1],
                           bias=self.nbias[:, t:t + 1]).then_inc(self.xn_ready, 1)

    def pe_transpose(self, pe, k, ident, src=None):
        src = self.xn if src is None else src
        for ch in range(KC):
            for t in range(TPC):
                if ch == 0:
                    pe.wait_ge(self.xn_ready, k * TPC + t + 1)
                last = pe.transpose(self.banks["T"][ch][:, t * P:(t + 1) * P],
                                    src[:, t, ch * P:(ch + 1) * P], ident[:])
            last.then_inc(self.t_ready, 1)

    def act_high(self, act, k):
        for ch in range(KC):
            act.wait_ge(self.t_ready, k * KC + ch + 1)
            act.copy(self.xh[:, ch, :], self.banks["T"][ch][:]).then_inc(self.xh_ready, 1)

    def dve_low(self, dve, k):
        for ch in range(KC):
            dve.wait_ge(self.xh_ready, k * KC + ch + 1)
            dve.tensor_tensor(self.xl[:, ch, :], self.banks["T"][ch][:], self.xh[:, ch, :].bitcast(F32),
                              ALU.subtract).then_inc(self.xl_ready, 1)

    def tile(self, t):
        cols = slice(t * P, (t + 1) * P)
        return [self.xh[:, ch, cols] for ch in range(KC)], [self.xl[:, ch, cols] for ch in range(KC)]

    def whole(self):
        return [self.xh[:, ch, :] for ch in range(KC)], [self.xl[:, ch, :] for ch in range(KC)]


class Experts:

    def __init__(self, ar, name, w, banks, ln):
        self.w, self.banks, self.ln = w, banks, ln
        sb, sem = (lambda n, s, d=F32: ar.sb(f"{name}_{n}", s, d)), (lambda n: ar.sem(f"{name}_{n}"))
        self.xb = sb("xb", [P, TPC, E])
        self.acc = sb("acc", [P, TPC, E])
        self.yl = sb("yl", [P, TPC, YL])
        self.lmax = sb("lmax", [P, TPC])
        self.dl = sb("dl", [P, TPC, NEXP])
        self.ex = sb("ex", [P, TPC, 8])
        self.top = sb("top", [P, TPC, 8])
        self.den = sb("den", [P, TPC])
        self.rden = sb("rden", [P, TPC])
        self.w2 = sb("w2", [P, TPC, 2])
        self.wsum = sb("wsum", [P, TPC])
        self.ffn_ready = sem("ffn_ready")
        self.yl_ready = sem("yl_ready")
        self.acc_ready = sem("acc_ready")
        self.xb_ready = sem("xb_ready")
        self.gate_chain = sem("gate_chain")
        self.ex_ready = sem("ex_ready")
        self.out_ready = sem("out_ready")

    def pe_tile(self, pe, k, t):
        n = k * TPC + t
        sh, ex = self.banks["F"][t % 2]
        if t == 0:
            pe.wait_ge(self.ln.xl_ready, k * KC + KC)
        if not (k is FIRST and t < 2):
            pe.wait_ge(self.yl_ready, n - 1)
            pe.wait_ge(self.acc_ready, n - 1)
        lh, ll = self.ln.tile(t)
        wh, wl = self.w
        cols = slice(W_EX, W_EX + YL)
        project(pe, ex[:, 0:YL], lh, ll, [wh[:, ch, cols] for ch in range(KC)], [wl[:, ch, cols] for ch in range(KC)])
        cols = slice(W_SH, W_SH + E)
        project(pe, sh[:, 0:E], lh, ll, [wh[:, ch, cols] for ch in range(KC)],
                [wl[:, ch, cols] for ch in range(KC)]).then_inc(self.ffn_ready, 1)

    def act_tile(self, act, k, t, first=False):
        act.wait_ge(self.ffn_ready, k * TPC + t + 1)
        if t == 0 and not first:
            act.wait_ge(self.out_ready, k * TPC)
        act.mul(self.yl[:, t, :], self.banks["F"][t % 2][1][:, 0:YL], 0.5).then_inc(self.yl_ready, 1)

    def dve_tile(self, dve, k, t):
        dve.wait_ge(self.ffn_ready, k * TPC + t + 1)
        dve.wait_ge(self.xb_ready, k * TPC + t + 1)
        dve.scalar_tensor_tensor(out=self.acc[:, t, :], in0=self.banks["F"][t % 2][0][:, 0:E], scalar=0.5,
                                 in1=self.xb[:, t, :], op0=ALU.mult, op1=ALU.add).then_inc(self.acc_ready, 1)

    def dve_logits(self, dve, k):
        ch = Chain(dve, self.gate_chain, k * GATE_LINKS)
        dve.wait_ge(self.yl_ready, k * TPC + TPC)
        logits = self.yl[:, :, E:E + NEXP]
        ch(dve.tensor_reduce(self.lmax[:], logits, AX.X, ALU.max))
        ch(dve.tensor_tensor(self.dl[:], logits, self.lmax[:].unsqueeze(2).to_broadcast([P, TPC, NEXP]), ALU.subtract))

    def dve_gate(self, dve, k):
        ch = Chain(dve, self.gate_chain, k * GATE_LINKS)
        ch.n = 2
        dve.wait_ge(self.ex_ready, k + 1)
        self.ln.hold.dve(dve, 2)
        for t in range(TPC):
            last = dve.max(self.top[:, t, :], self.ex[:, t, :])
            if t < TPC - 1:
                last.then_inc(self.gate_chain, 1)
                ch.n += 1
        ch(last)
        ch(dve.tensor_tensor(self.den[:], self.top[:, :, 0], self.top[:, :, 1], ALU.add))
        ch(dve.reciprocal(self.rden[:], self.den[:]))
        ch(dve.tensor_tensor(self.w2[:], self.top[:, :, 0:2], self.rden[:].unsqueeze(2).to_broadcast([P, TPC, 2]), ALU.mult))
        ch(dve.tensor_tensor(self.wsum[:], self.w2[:, :, 0], self.w2[:, :, 1], ALU.add))
        assert ch.n == GATE_LINKS

    def act_exp(self, act, k):
        act.wait_ge(self.gate_chain, k * GATE_LINKS + 2)
        act.activation(self.ex[:, :, 0:NEXP], self.dl[:], ACT.Exp, scale=2.0).then_inc(self.ex_ready, 1)

    def dve_out(self, dve, k, t, out):
        if t == 0:
            dve.wait_ge(self.acc_ready, k * TPC + TPC)
        dve.scalar_tensor_tensor(out=out[:, t, :], in0=self.yl[:, t, 0:E], scalar=self.wsum[:, t:t + 1],
                                 in1=self.acc[:, t, :], op0=ALU.mult, op1=ALU.add).then_inc(self.out_ready, 1)

    def pool_xb(self, pool, k, x, hbias, first=False):
        if not first:
            pool.wait_ge(self.acc_ready, k * TPC)
        for t in range(TPC):
            pool.tensor_tensor(self.xb[:, t, :], x[:, t, :], hbias[:], ALU.add).then_inc(self.xb_ready, 1)


class _First(int):
    pass


FIRST = _First(0)


def stage_a(nc, psum, const, io, scratch):
    ident, mhalf, zero, hbias, wh, wl, hold = const
    with ExitStack() as ctx:
        ar = Arena(nc, ctx, hold)
        banks = {"T": psum[0:2], "F": [psum[2:4], psum[4:6]], "Q": psum[6:8]}
        x = ar.sb("a_x", [P, TPC, E])
        x1 = ar.sb("a_x1", [P, TPC, E])
        qk = ar.sb("a_qk", [P, 2 * KC, 2, CHUNK], F32R)
        v = ar.sb("a_v", [P, TPC, E])
        stage = ar.sb("a_stage", [P, KC, WCOLS])
        brow = ar.sb("a_brow", [P, E])
        ln1 = Ffn(ar, "a_ln1", (wh, wl), banks, zero)
        ln2 = Ffn(ar, "a_ln2", (wh, wl), banks, zero, 1)
        ffn = Experts(ar, "a_ffn", (wh, wl), banks, ln1)
        w_loaded = ar.sem("w_loaded")
        pad_ready = ar.sem("pad_ready")
        w_ready = ar.sem("w_ready")
        b_ready = ar.sem("b_ready")
        c_ready = ar.sem("c_ready")
        x_loaded = ar.sem("x_loaded")
        x1_stored = ar.sem("x1_stored")
        qk_stored = ar.sem("qk_stored")
        v_stored = ar.sem("v_stored")
        qkv_ready = ar.sem("qkv_ready")
        qh_ready = ar.sem("qh_ready")
        ql_ready = ar.sem("ql_ready")
        NQK, QKV = 2 * KC, 2 * KC + TPC // 2
        PROJ = [("qk", 0), ("qk", 1), ("v", 0), ("v", 1), ("qk", 2), ("qk", 3)]
        PROJ_EARLY = 3
        proj_bank = [*banks["F"][0], *banks["F"][1], *banks["Q"]]

        block = ctx.enter_context(nc.Block())

        @block.sync
        def _(sp):
            for src, col in io["weights"]:
                n = src.shape[1]
                sp.dma_start(stage[:, :, col:col + n], src.rearrange("(k p) n -> p k n", p=P)).then_inc(w_loaded, 16)
            sp.dma_start(brow[:], io["bias"].rearrange("(a n) -> a n", a=1).to_broadcast([P, E])).then_inc(w_loaded, 16)

            def load(c):
                sp.dma_start(x[:], io["x"][bass.ds(c, 1)].rearrange("a p t e -> p (a t) e")).then_inc(x_loaded, 16)

            def store_x1(c):
                sp.wait_ge(ffn.out_ready, c * TPC + TPC)
                sp.dma_start(scratch["x1"][bass.ds(c, 1)].rearrange("a p t e -> p (a t) e"), x1[:]).then_inc(x1_stored, 16)

            def store_qkv(c):
                for j in range(NQK):
                    sp.wait_ge(ql_ready, c * NQK + j + 1)
                    dst = scratch["qk"][bass.ds(c // 2, 1), j // KC, :, (j % KC) * P:(j % KC + 1) * P, bass.ds(c % 2, 1)]
                    sp.dma_start(dst.rearrange("a q r f n -> r (a q) (f n)"), qk[:, j, :, :].bitcast(F32)).then_inc(qk_stored, 16)
                sp.wait_ge(qh_ready, c * QKV + QKV)
                sp.dma_start(scratch["v"][bass.ds(c, 1)].rearrange("a t p e -> p (a t) e"), v[:]).then_inc(v_stored, 16)

            def step(c, prev, nxt2):
                if nxt2:
                    sp.wait_ge(ln1.xn_ready, c * TPC + 2 * TPC)
                    sp.wait_ge(ffn.xb_ready, c * TPC + 2 * TPC)
                    load(c + 2)
                store_x1(c)
                if prev:
                    store_qkv(c - 1)

            load(0)
            sp.wait_ge(ln1.xn_ready, TPC)
            sp.wait_ge(ffn.xb_ready, TPC)
            load(1)
            step(0, False, True)
            with sp.Fori(1, NCHUNK - 2) as c:
                step(c, True, True)
            step(NCHUNK - 2, True, False)
            step(NCHUNK - 1, True, False)
            store_qkv(NCHUNK - 1)
            sp.wait_ge(x1_stored, NCHUNK * 16)
            sp.wait_ge(qk_stored, NCHUNK * NQK * 16)
            sp.wait_ge(v_stored, NCHUNK * 16)

        @block.gpsimd
        def _(pool):
            pool.memset(ident[:], 0.0).then_inc(c_ready, 1)
            pool.memset(mhalf[:], -0.5).then_inc(c_ready, 1)
            pool.memset(zero[:], 0.0).then_inc(c_ready, 1)
            pool.memset(ffn.ex[:], 0.0).then_inc(c_ready, 1)
            pool.memset(stage[:, :, W_EX + E + NEXP:W_EX + YL], 0.0).then_inc(pad_ready, 1)
            pool.wait_ge(c_ready, 4)
            pool.affine_select(out=ident[:], in_=ident[:], compare_op=ALU.not_equal, fill=1.0, base=0,
                               pattern=[[-1, P]], channel_multiplier=1).then_inc(c_ready, 1)
            pool.wait_ge(x_loaded, 16)
            pool.wait_ge(b_ready, 1)
            ln1.pool_rstd(pool, 0, mhalf, first=True)
            ffn.pool_xb(pool, 0, x, hbias, first=True)

            def step(c, nxt):
                if nxt:
                    ln1.pool_rstd(pool, c + 1, mhalf)
                    ffn.pool_xb(pool, c + 1, x, hbias)
                ln2.pool_rstd(pool, c, mhalf, first=(c is FIRST))

            step(FIRST, True)
            with pool.Fori(1, NCHUNK - 1) as c:
                step(c, True)
            step(NCHUNK - 1, False)

        @block.scalar
        def _(act):
            act.preload_act_table(ACT.Exp)
            act.wait_ge(x_loaded, 16)
            ln1.act_normalise(act, 0, x, first=True)
            ln1.act_high(act, 0)

            def high(c, j, first):
                kind, i = PROJ[j]
                act.wait_ge(qkv_ready, c * QKV + j + 1)
                if kind == "v":
                    if not first:
                        act.wait_ge(v_stored, c * 16)
                    act.copy(v[:, 2 * i:2 * i + 2, :], proj_bank[j][:].rearrange("p (t e) -> p t e", t=2)).then_inc(qh_ready, 1)
                else:
                    if not first:
                        act.wait_ge(qk_stored, c * NQK * 16)
                    act.mul(qk[:, i, 0, :], proj_bank[j][:], 0.25 if i < KC else 1.0).then_inc(qh_ready, 1)

            def step(c, prev, nxt, prev_first=False):
                first = c is FIRST

                def norm2(*tiles):
                    if prev:
                        ln2.act_normalise(act, FIRST if prev_first else c - 1, x1, prev_first, tiles)

                def norm1(*tiles):
                    if nxt:
                        ln1.act_normalise(act, c + 1, x, False, tiles)

                norm2(0)
                ffn.act_tile(act, c, 0, first)
                norm2(1, 2)
                ffn.act_tile(act, c, 1)
                norm2(3)
                ffn.act_tile(act, c, 2)
                if prev:
                    ln2.act_high(act, c - 1)
                norm1(0)
                ffn.act_tile(act, c, 3)
                norm1(1)
                ffn.act_exp(act, c)
                norm1(2, 3)
                if prev:
                    for j in range(PROJ_EARLY):
                        high(c - 1, j, prev_first)
                if nxt:
                    ln1.act_high(act, c + 1)
                if prev:
                    for j in range(PROJ_EARLY, QKV):
                        high(c - 1, j, prev_first)

            step(FIRST, False, True)
            step(1, True, True, True)
            with act.Fori(2, NCHUNK - 1) as c:
                step(c, True, True)
            step(NCHUNK - 1, True, False)
            ln2.act_normalise(act, NCHUNK - 1, x1)
            ln2.act_high(act, NCHUNK - 1)
            for j in range(QKV):
                high(NCHUNK - 1, j, False)

        @block.vector
        def _(dve):
            dve.wait_ge(w_loaded, 16 * (len(io["weights"]) + 1))
            dve.wait_ge(pad_ready, 1)
            dve.tensor_scalar(hbias[:], brow[:], 0.5, None, ALU.mult).then_inc(b_ready, 1)
            dve.tensor_copy(wh[:], stage[:]).then_inc(w_ready, 1)
            dve.wait_ge(w_ready, 1)
            dve.tensor_tensor(wl[:], stage[:], wh[:].bitcast(F32), ALU.subtract).then_inc(w_ready, 1)

            def low(c, i):
                j = PROJ.index(("qk", i))
                dve.wait_ge(qh_ready, c * QKV + j + 1)
                dve.scalar_tensor_tensor(out=qk[:, i, 1, :], in0=proj_bank[j][:], scalar=0.25 if i < KC else 1.0,
                                         in1=qk[:, i, 0, :].bitcast(F32), op0=ALU.mult,
                                         op1=ALU.subtract).then_inc(ql_ready, 1)

            def step(c, prev, nxt):
                ffn.dve_tile(dve, c, 0)
                if nxt:
                    dve.wait_ge(x_loaded, c * 16 + 32)
                    for t in (0, 1):
                        ln1.dve_stats(dve, c + 1, t, x)
                ffn.dve_tile(dve, c, 1)
                if nxt:
                    for t in (2, 3):
                        ln1.dve_stats(dve, c + 1, t, x)
                    ln1.dve_aggregate(dve, c + 1)
                ffn.dve_tile(dve, c, 2)
                if prev:
                    ln2.dve_low(dve, c - 1)
                ffn.dve_tile(dve, c, 3)
                ffn.dve_logits(dve, c)
                ffn.dve_gate(dve, c)
                if prev:
                    low(c - 1, 0)
                    dve.wait_ge(x1_stored, c * 16)
                    dve.wait_ge(ln2.xn_ready, c * TPC)
                for t in range(TPC):
                    ffn.dve_out(dve, c, t, x1)
                    if t:
                        dve.wait_ge(ffn.out_ready, c * TPC + t)
                        ln2.dve_stats(dve, c, t - 1, x1)
                dve.wait_ge(ffn.out_ready, c * TPC + TPC)
                ln2.dve_stats(dve, c, TPC - 1, x1)
                ln2.dve_aggregate(dve, c, first=(c is FIRST))
                if prev:
                    low(c - 1, 1)
                if nxt:
                    ln1.dve_low(dve, c + 1)
                if prev:
                    low(c - 1, 2)
                    low(c - 1, 3)

            dve.wait_ge(x_loaded, 16)
            for t in range(TPC):
                ln1.dve_stats(dve, 0, t, x)
            ln1.dve_aggregate(dve, 0, first=True)
            ln1.dve_low(dve, 0)
            step(FIRST, False, True)
            with dve.Fori(1, NCHUNK - 1) as c:
                step(c, True, True)
            step(NCHUNK - 1, True, False)
            ln2.dve_low(dve, NCHUNK - 1)
            for i in range(NQK):
                low(NCHUNK - 1, i)

        @block.tensor
        def _(pe):
            def qkv(c, js, first=False, last=False):
                th, tl = ln2.whole()
                for j in js:
                    kind, i = PROJ[j]
                    if j == 0:
                        pe.wait_ge(ln2.xl_ready, c * KC + KC)
                    if last:
                        pe.wait_ge(ql_ready, c * NQK)
                        pe.wait_ge(qh_ready, c * QKV)
                    elif j in (0, 2):
                        pe.wait_ge(ffn.yl_ready, c * TPC + TPC + 3 + j // 2)
                        pe.wait_ge(ffn.acc_ready, c * TPC + TPC + 3 + j // 2)
                    elif j == 4 and not first:
                        pe.wait_ge(ql_ready, c * NQK)
                    bank = proj_bank[j]
                    if kind == "qk":
                        cols = slice(W_QK + i * P, W_QK + (i + 1) * P)
                        project(pe, bank[:], [wh[:, ch, cols] for ch in range(KC)], [wl[:, ch, cols] for ch in range(KC)],
                                th, tl).then_inc(qkv_ready, 1)
                    else:
                        cols = slice(W_V, W_V + E)
                        for t in (2 * i, 2 * i + 1):
                            lh, ll = ln2.tile(t)
                            done = project(pe, bank[:, (t % 2) * E:(t % 2 + 1) * E], lh, ll,
                                           [wh[:, ch, cols] for ch in range(KC)], [wl[:, ch, cols] for ch in range(KC)])
                        done.then_inc(qkv_ready, 1)

            def step(c, prev, nxt, prev_first=False):
                if prev and not prev_first:
                    pe.wait_ge(ql_ready, c * NQK - 2 * NQK + 2)
                ffn.pe_tile(pe, c, 0)
                if prev and not prev_first:
                    pe.wait_ge(qh_ready, c * QKV - 2 * QKV + 4)
                ffn.pe_tile(pe, c, 1)
                ffn.pe_tile(pe, c, 2)
                if prev:
                    ln2.pe_transpose(pe, c - 1, ident)
                ffn.pe_tile(pe, c, 3)
                if prev:
                    qkv(c - 1, range(PROJ_EARLY), prev_first)
                if nxt:
                    ln1.pe_transpose(pe, c + 1, ident)
                if prev:
                    qkv(c - 1, range(PROJ_EARLY, QKV), prev_first)

            pe.wait_ge(c_ready, 5)
            pe.wait_ge(w_ready, 2)
            ln1.pe_transpose(pe, 0, ident)
            step(FIRST, False, True)
            step(1, True, True, True)
            with pe.Fori(2, NCHUNK - 1) as c:
                step(c, True, True)
            step(NCHUNK - 1, True, False)
            ln2.pe_transpose(pe, NCHUNK - 1, ident)
            qkv(NCHUNK - 1, range(QKV), last=True)


def stage_b(nc, psum, const, scratch):
    ident, _, zero, *_, hold = const
    with ExitStack() as ctx:
        ar = Arena(nc, ctx, hold)
        s_bank, m_bank, o_bank = psum[0:SB], psum[SB:2 * SB], psum[2 * SB:2 * SB + 2]
        qs = [ar.sb(f"b_qs{n}", [P, GH, T], F32R) for n in range(NBUF)]
        ks = [ar.sb(f"b_ks{n}", [P, GH, T], F32R) for n in range(NBUF)]
        vx = [ar.sb(f"b_vx{n}", [P, KT, GH, 2 * D]) for n in range(NBUF)]
        vin = ar.sb("b_vin", [P, KT, GH * D])
        probs = ar.sb("b_probs", [P, NBUF, GH, BANK])
        o = ar.sb("b_o", [P, 2, BANK])
        mask = ar.sb("b_mask", [P, BANK])
        junk = ar.sb("b_junk", [P, SB, BANK], BF16)
        rest = ar.sb("b_rest", [P, T])
        pm = ar.sb("b_pm", [P, 2, GH, KT])
        mparts = ar.sb("b_mparts", [P, P // (GH * KT), GH * KT], F32R)
        mt = ar.sb("b_mt", [2 * GH * KT, P], F32R)

        c_ready = ar.sem("b_c_ready")
        z_ready = ar.sem("b_z_ready")
        qz_ready = ar.sem("b_qz_ready")
        kz_ready = ar.sem("b_kz_ready")
        stacked = [ar.sem(f"b_stacked{n}") for n in range(NBUF)]
        v_loaded = ar.sem("b_v_loaded")
        vx_ready = ar.sem("b_vx_ready")
        m_tile = ar.sem("b_m_tile")
        m_read = ar.sem("b_m_read")
        m_chain = ar.sem("b_m_chain")
        m_turned = ar.sem("b_m_turned")
        m_out = ar.sem("b_m_out")
        m_placed = [ar.sem(f"b_m_placed{n}") for n in range(NBUF)]
        s_tile = ar.sem("b_s_tile")
        p_ready = ar.sem("b_p_ready")
        p_masked = ar.sem("b_p_masked")
        pv_done = ar.sem("b_pv_done")
        o_out = ar.sem("b_o_out")
        o_stored = [ar.sem(f"b_o_stored{n}") for n in range(2)]
        STACK = 16 * 8
        ND = len(DIAG_SLOTS)

        class Group:

            def __init__(self, r, k):
                if isinstance(r, int):
                    r, k = 0, NBUF * r + k
                self.r, self.k, self.buf = r, k, k % NBUF

            def at(self, per, more=0):
                return self.r * (NBUF * per) + (self.k * per + more)

            def turn(self, per, more=0):
                return self.r * per + (self.k // NBUF * per + more)

            def next(self, n):
                return Group(self.r, self.k + n) if not isinstance(self.r, int) else Group(0, self.k + n)

            @property
            def first(self):
                return isinstance(self.r, int) and self.k == 0

        def groups(eng, step):
            step(Group(0, 0), False)
            with eng.Fori(0, (NG - 2) // NBUF) as r:
                for k in range(1, NBUF + 1):
                    step(Group(r, k), False)
            step(Group(0, NG - 1), True)

        assert (NG - 2) % NBUF == 0
        block = ctx.enter_context(nc.Block())

        @block.sync
        def _(sp):
            def load(g):
                i = g.at(1) % NG
                b, gg = i // GPB, i % GPB
                for kind, dst, order in ((0, qs[g.buf], (0, 0, 1, 1)), (1, ks[g.buf], (0, 1, 0, 1))):
                    for n, part in enumerate(order):
                        src = scratch["qk_b"][bass.ds(b, 1), kind, part, bass.ds(gg, 1)]
                        sp.dma_start(dst[n * D:(n + 1) * D, :, :].bitcast(F32),
                                     src.rearrange("a g h d n -> d (a g h) n")).then_inc(stacked[g.buf], 16)

            def load_v(g):
                i = g.at(1)
                b, gg = i // GPB, i % GPB
                sp.dma_start(vin[:], scratch["v_b"][bass.ds(b, 1), :, :, bass.ds(gg, 1)].rearrange(
                    "a k p g n -> p (a k) (g n)")).then_inc(v_loaded, 16)

            def place_m(g):
                sp.wait_ge(m_out, g.at(1, 1))
                sp.dma_start(qs[g.buf][SROWS:SROWS_M, :, :].rearrange("r h (i p) -> r (h i) p", p=P).bitcast(F32),
                             mt[:].bitcast(F32)).then_inc(m_placed[g.buf], 16)

            def store(g, half):
                sp.wait_ge(o_out, g.at(2, half + 1))
                sp.dma_start(scratch["o"][bass.ds(g.at(1), 1), :, half].rearrange("a r n -> (a r) n"),
                             o[:, half, :]).then_inc(o_stored[half], 16)

            load(Group(0, 0))
            load(Group(0, 1))
            load_v(Group(0, 0))
            sp.wait_ge(qz_ready, NBUF)
            place_m(Group(0, 0))

            def step(g, last):
                if not last:
                    if not g.first:
                        sp.wait_ge(s_tile, g.at(TILES))
                    load(g.next(2))
                    sp.wait_ge(vx_ready, g.at(1, 1))
                    load_v(g.next(1))
                if not g.first:
                    store(g.next(-1), 1)
                if not last:
                    place_m(g.next(1))
                store(g, 0)

            groups(sp, step)
            store(Group(0, NG - 1), 1)
            for half in range(2):
                sp.wait_ge(o_stored[half], 16 * NG)

        @block.gpsimd
        def _(pool):
            setup = Chain(pool, c_ready, 0)
            setup(pool.memset(rest[SROWS:P, :], 0.0))
            setup(pool.memset(rest[SROWS:SROWS_M, :], 1.0))
            setup(pool.memset(mask[:], 0.0))
            diag = mask[:, BANK - P:BANK]
            setup(pool.affine_select(out=diag, in_=diag, compare_op=ALU.is_ge, fill=MASKED, base=0,
                                     pattern=[[-1, P]], channel_multiplier=1))
            clear = Chain(pool, qz_ready, 0)
            for n in range(NBUF):
                clear(pool.memset(qs[n][SROWS:P, :, :].bitcast(F32), 0.0))
                setup(pool.memset(vx[n][:], 1.0))

            def expand_v(g):
                pool.wait_ge(v_loaded, g.at(16, 16))
                hold.pool(pool, ND, zero)
                pool.tensor_copy(vx[g.buf][:, :, :, 0:D],
                                 vin[:].rearrange("p k (h d) -> p k h d", h=GH)).then_inc(vx_ready, 1)

            def step(g, last):
                for s in DIAG_SLOTS:
                    pool.wait_ge(p_ready, g.at(TILES, GH * (s + 1)))
                    hold.pool(pool, DIAG_SLOTS.index(s), zero)
                    for n, off in enumerate(DIAG[s]):
                        blk = probs[:, s % NBUF, :, off:off + P]
                        ins = pool.affine_select(out=blk, in_=blk, compare_op=ALU.is_ge, fill=0.0, base=0,
                                                 pattern=[[0, GH], [1, P]], channel_multiplier=-1)
                    ins.then_inc(p_masked, 1)
                    if s == LOW_DONE and not last:
                        expand_v(g.next(1))

            expand_v(Group(0, 0))
            groups(pool, step)

        @block.scalar
        def _(act):
            def out_m(g):
                act.wait_ge(m_turned, g.at(1, 1))
                if not g.first:
                    p = g.next(-1)
                    act.wait_ge(m_placed[p.buf], p.turn(16, 16))
                act.copy(mt[:], m_bank[M_BANK][0:2 * GH * KT, 0:P]).then_inc(m_out, 1)

            def out_o(g, half):
                act.wait_ge(pv_done, g.at(NSLOT, (LOW_DONE, HIGH_DONE)[half] + 1))
                if not g.first:
                    act.wait_ge(o_stored[half], g.at(16))
                act.copy(o[:, half, :], o_bank[half][:]).then_inc(o_out, 1)

            def exp(g, s):
                if not (g.first and s < NBUF):
                    act.wait_ge(pv_done, g.at(NSLOT, s - NBUF + 1))
                for h in range(GH):
                    t = s * GH + h
                    act.wait_ge(s_tile, g.at(TILES, t + 1))
                    act.activation(probs[:, s % NBUF, h, :], s_bank[t % SB][:], ACT.Exp).then_inc(p_ready, 1)

            def step(g, last):
                for s in range(NSLOT):
                    exp(g, s)
                    if s == 2 and not g.first:
                        out_o(g.next(-1), 1)
                    if s == NSLOT - AHEAD and not last:
                        out_m(g.next(1))
                    if s == LOW_DONE + 3:
                        out_o(g, 0)

            act.wait_ge(c_ready, 2)
            for n in range(NBUF):
                for h in range(GH):
                    act.copy(ks[n][SROWS:P, h, :], rest[SROWS:P, :]).then_inc(kz_ready, 1)
            out_m(Group(0, 0))
            groups(act, step)
            out_o(Group(0, NG - 1), 1)

        @block.vector
        def _(dve):
            dve.memset(mparts[:].bitcast(F32), 0.0).then_inc(z_ready, 1)
            dve.wait_ge(z_ready, 1)
            dve.wait_ge(c_ready, 4)

            def maxima(g, a):
                for h in range(GH):
                    t = a * GH + h
                    dve.wait_ge(m_tile, g.at(TILES, t + 1))
                    if not (g.first and t < SB):
                        dve.wait_ge(m_read, g.at(TILES, t - SB + 1))
                    hold.dve(dve, t % 4)
                    bank = m_bank[t % SB]
                    for i, k0, n, off in MAX_SLOTS[a]:
                        src = bank[:, off:off + n]
                        if k0 + n == (i + 1) * P:
                            ins = dve.tensor_tensor_reduce(junk[:, t % SB, off:off + n], src, mask[:, BANK - n:BANK], 1.0, 0.0, ALU.add,
                                                           ALU.max, pm[:, 0, h, i:i + 1])
                        else:
                            ins = dve.tensor_reduce(pm[:, 1, h, i:i + 1], src, AX.X, ALU.max)
                    ins.then_inc(m_read, 1)

            def parts(g):
                ch = Chain(dve, m_chain, g.at(3))
                dve.wait_ge(m_read, g.at(TILES, TILES))
                if not g.first:
                    dve.wait_ge(m_turned, g.at(1))
                two = slice(KT // 2, KT)
                ch(dve.tensor_tensor(pm[:, 0, :, two], pm[:, 0, :, two], pm[:, 1, :, two], ALU.max))
                whole = pm[:, 0, :, :].rearrange("p h i -> p (h i)")
                ch(dve.tensor_scalar(mparts[:, 0, :], whole, -1.0, None, ALU.mult))
                ch(dve.scalar_tensor_tensor(out=mparts[:, 1, :], in0=whole, scalar=-1.0,
                                            in1=mparts[:, 0, :].bitcast(F32), op0=ALU.mult, op1=ALU.subtract))

            def step(g, last):
                if last:
                    return
                for a in range(AHEAD, NSLOT):
                    maxima(g.next(1), a)
                parts(g.next(1))
                for a in range(AHEAD):
                    maxima(g.next(2), a)

            for a in range(NSLOT):
                maxima(Group(0, 0), a)
            parts(Group(0, 0))
            for a in range(AHEAD):
                maxima(Group(0, 1), a)
            groups(dve, step)

        @block.tensor
        def _(pe):
            def turn_m(g):
                pe.wait_ge(m_chain, g.at(3, 3))
                pe.wait_ge(m_read, g.at(TILES, TILES + M_BANK + 1))
                pe.transpose(m_bank[M_BANK][:, 0:P],
                             mparts[:].rearrange("p q n -> p (q n)").bitcast(F32), ident[:]).then_inc(m_turned, 1)

            def max_tile(g, a, h):
                t = a * GH + h
                if t == 0:
                    pe.wait_ge(stacked[g.buf], g.turn(STACK, STACK))
                if not (g.first and t < SB):
                    pe.wait_ge(m_read, g.at(TILES, t - SB + 1))
                if t == GH and not g.first:
                    pe.wait_ge(m_out, g.at(1))
                for i, k0, n, off in MAX_SLOTS[a]:
                    last = pe.matmul(m_bank[t % SB][:, off:off + n], qs[g.buf][0:SROWS, h, i * P:(i + 1) * P],
                                     ks[g.buf][0:SROWS, h, k0:k0 + n], start=True, stop=True)
                last.then_inc(m_tile, 1)

            def score_tile(g, s, h):
                t = s * GH + h
                if t == 0:
                    pe.wait_ge(m_placed[g.buf], g.turn(16, 16))
                if not (g.first and t < SB):
                    pe.wait_ge(p_ready, g.at(TILES, t - SB + 1))
                for j, q0, n, off in SLOTS[s]:
                    last = pe.matmul(s_bank[t % SB][:, off:off + n], ks[g.buf][:, h, j * P:(j + 1) * P],
                                     qs[g.buf][:, h, q0:q0 + n], start=True, stop=True)
                last.then_inc(s_tile, 1)

            def values(g, s):
                pe.wait_ge(p_ready, g.at(TILES, GH * (s + 1)))
                if DIAG[s]:
                    pe.wait_ge(p_masked, g.at(ND, DIAG_SLOTS.index(s) + 1))
                if s == 0:
                    pe.wait_ge(vx_ready, g.at(1, 1))
                if s < 2 and not g.first:
                    pe.wait_ge(o_out, g.at(2, s - 1))
                for j, q0, n, off in SLOTS[s]:
                    half, col = q0 // BANK, q0 % BANK
                    for h in range(GH):
                        last = pe.matmul(o_bank[half][2 * D * h:2 * D * (h + 1), col:col + n], vx[g.buf][:, j, h, :],
                                         probs[:, s % NBUF, h, off:off + n], start=(j == 0),
                                         stop=(s in (LOW_DONE, HIGH_DONE) and half == (s == HIGH_DONE)),
                                         tile_position=(0, 2 * D * h))
                last.then_inc(pv_done, 1)

            def step(g, last):
                for s in range(NSLOT):
                    for h in range(GH):
                        score_tile(g, s, h)
                        if not last:
                            a = s + AHEAD
                            if a < NSLOT:
                                max_tile(g.next(1), a, h)
                            else:
                                max_tile(g.next(2), a - NSLOT, h)
                    if s == NSLOT - AHEAD and not last:
                        turn_m(g.next(1))
                    if s >= 2:
                        values(g, s - 2)
                    elif not g.first:
                        values(g.next(-1), NSLOT - 2 + s)

            for a in range(NSLOT):
                for h in range(GH):
                    max_tile(Group(0, 0), a, h)
            for a in range(AHEAD):
                for h in range(GH):
                    max_tile(Group(0, 1), a, h)
                if a == 0:
                    turn_m(Group(0, 0))
            pe.wait_ge(kz_ready, NBUF * GH)
            pe.wait_ge(qz_ready, NBUF)
            groups(pe, step)
            for s in (NSLOT - 2, NSLOT - 1):
                values(Group(0, NG - 1), s)


def stage_c(nc, psum, const, io, scratch):
    ident, mhalf, zero, hbias, wh, wl, hold = const
    with ExitStack() as ctx:
        ar = Arena(nc, ctx, hold)
        banks = {"T": psum[0:2], "F": [psum[2:4], psum[4:6]]}
        o_bank = psum[6:8]
        ot = ar.sb("c_ot", [P, GPB, CHUNK])
        on = ar.sb("c_on", [P, TPC, E])
        rden = ar.sb("c_rden", [P, TPC, H])
        oh = ar.sb("c_oh", [P, KC, CHUNK], F32R)
        ol = ar.sb("c_ol", [P, KC, CHUNK], F32R)
        x1 = ar.sb("c_x1", [P, TPC, E])
        x2 = ar.sb("c_x2", [P, TPC, E])
        out = ar.sb("c_out", [P, TPC, E])
        ln = Ffn(ar, "c_ln", (wh, wl), banks, zero)
        ffn = Experts(ar, "c_ffn", (wh, wl), banks, ln)
        ot_loaded = ar.sem("c_ot_loaded")
        x1_loaded = ar.sem("c_x1_loaded")
        o_turned = ar.sem("c_o_turned")
        r_ready = ar.sem("c_r_ready")
        on_ready = ar.sem("c_on_ready")
        ot_ready = ar.sem("c_ot_ready")
        oh_ready = ar.sem("c_oh_ready")
        ol_ready = ar.sem("c_ol_ready")
        op_ready = ar.sem("c_op_ready")
        x2_ready = ar.sem("c_x2_ready")
        stored = ar.sem("c_stored")
        c_ready = ar.sem("c_c_ready")

        block = ctx.enter_context(nc.Block())

        @block.sync
        def _(sp):
            def load_o(c):
                b, half = c // 2, c % 2
                sp.dma_start(ot[:], scratch["o_b"][bass.ds(b, 1), :, :, bass.ds(half, 1)].rearrange(
                    "a g r f n -> r (a g) (f n)")).then_inc(ot_loaded, 16)

            def load_x1(c):
                sp.dma_start(x1[:], scratch["x1"][bass.ds(c, 1)].rearrange("a p t e -> p (a t) e")).then_inc(x1_loaded, 16)

            def store(c):
                sp.wait_ge(ffn.out_ready, c * TPC + TPC)
                sp.dma_start(io["out"][bass.ds(c, 1)].rearrange("a p t e -> p (a t) e"), out[:]).then_inc(stored, 16)

            def step(c, prev, nxt, nxt2):
                if nxt2:
                    sp.wait_ge(o_turned, c * TPC + 2 * TPC)
                    load_o(c + 2)
                if nxt:
                    sp.wait_ge(x2_ready, c * TPC + TPC)
                    load_x1(c + 1)
                if prev:
                    store(c - 1)

            load_o(0)
            load_x1(0)
            sp.wait_ge(o_turned, TPC)
            load_o(1)
            step(0, False, True, True)
            with sp.Fori(1, NCHUNK - 2) as c:
                step(c, True, True, True)
            step(NCHUNK - 2, True, True, False)
            step(NCHUNK - 1, True, False, False)
            store(NCHUNK - 1)
            sp.wait_ge(stored, NCHUNK * 16)

        @block.gpsimd
        def _(pool):
            pool.memset(ffn.ex[:], 0.0).then_inc(c_ready, 1)

            def step(c, first=False):
                ln.pool_rstd(pool, c, mhalf, first)
                ffn.pool_xb(pool, c, x2, hbias, first)

            step(0, True)
            with pool.Fori(1, NCHUNK) as c:
                step(c)

        @block.scalar
        def _(act):
            act.wait_ge(c_ready, 1)

            def high(c):
                for ch in range(KC):
                    act.wait_ge(ot_ready, c * KC + ch + 1)
                    act.copy(oh[:, ch, :], banks["T"][ch][:]).then_inc(oh_ready, 1)

            def step(c, prev, prev_first=False):
                k = FIRST if prev_first else c - 1
                high(c)
                if prev:
                    ln.act_high(act, k)
                    for t in range(TPC):
                        ffn.act_tile(act, k, t, prev_first)
                    ffn.act_exp(act, k)
                ln.act_normalise(act, c, x2, first=not prev)

            step(0, False)
            step(1, True, True)
            with act.Fori(2, NCHUNK) as c:
                step(c, True)
            ln.act_high(act, NCHUNK - 1)
            for t in range(TPC):
                ffn.act_tile(act, NCHUNK - 1, t)
            ffn.act_exp(act, NCHUNK - 1)

        @block.vector
        def _(dve):
            def normalise(c, first=False):
                if not first:
                    dve.wait_ge(ot_ready, c * KC)
                for t in range(TPC):
                    dve.wait_ge(o_turned, c * TPC + t + 1)
                    heads = o_bank[t % 2][:].rearrange("p (h n) -> p h n", h=H)
                    dve.reciprocal(rden[:, t, :], heads[:, :, D]).then_inc(r_ready, 1)
                    dve.wait_ge(r_ready, c * TPC + t + 1)
                    dve.tensor_tensor(on[:, t, :].rearrange("p (h n) -> p h n", h=H), heads[:, :, 0:D],
                                      rden[:, t, :].unsqueeze(2).to_broadcast([P, H, D]), ALU.mult).then_inc(on_ready, 1)

            def low(c):
                for ch in range(KC):
                    dve.wait_ge(oh_ready, c * KC + ch + 1)
                    dve.tensor_tensor(ol[:, ch, :], banks["T"][ch][:], oh[:, ch, :].bitcast(F32),
                                      ALU.subtract).then_inc(ol_ready, 1)

            def residual(c, first):
                dve.wait_ge(x1_loaded, c * 16 + 16)
                if not first:
                    dve.wait_ge(ln.xn_ready, c * TPC)
                    dve.wait_ge(ffn.xb_ready, c * TPC)
                for t in range(TPC):
                    if t % 2 == 0:
                        dve.wait_ge(op_ready, c * TPC + t + 2)
                    dve.tensor_tensor(x2[:, t, :], o_bank[t // 2][:, (t % 2) * E:(t % 2 + 1) * E], x1[:, t, :],
                                      ALU.add).then_inc(x2_ready, 1)
                    if t:
                        dve.wait_ge(x2_ready, c * TPC + t)
                        ln.dve_stats(dve, c, t - 1, x2)
                dve.wait_ge(x2_ready, c * TPC + TPC)
                ln.dve_stats(dve, c, TPC - 1, x2)
                ln.dve_aggregate(dve, c, first)

            def finish(c, first):
                ffn.dve_logits(dve, c)
                ffn.dve_gate(dve, c)
                if not first:
                    dve.wait_ge(stored, c * 16)
                for t in range(TPC):
                    ffn.dve_out(dve, c, t, out)

            def step(c, prev, nxt, prev_first=False):
                low(c)
                if nxt:
                    normalise(c + 1)
                if prev:
                    ln.dve_low(dve, c - 1)
                residual(c, first=not prev)
                if prev:
                    for t in range(TPC):
                        ffn.dve_tile(dve, c - 1, t)
                    finish(c - 1, prev_first)

            normalise(0, first=True)
            step(0, False, True)
            step(1, True, True, True)
            with dve.Fori(2, NCHUNK - 1) as c:
                step(c, True, True)
            step(NCHUNK - 1, True, False)
            ln.dve_low(dve, NCHUNK - 1)
            for t in range(TPC):
                ffn.dve_tile(dve, NCHUNK - 1, t)
            finish(NCHUNK - 1, False)

        @block.tensor
        def _(pe):
            def turn(c, first=False):
                pe.wait_ge(ot_loaded, c * 16 + 16)
                for t in range(TPC):
                    if t >= 2:
                        pe.wait_ge(on_ready, c * TPC + t - 1)
                    elif first:
                        if c:
                            pe.wait_ge(on_ready, c * TPC)
                    else:
                        pe.wait_ge(x2_ready, c * TPC - TPC)
                    for g in range(GPB):
                        last = pe.transpose(o_bank[t % 2][:, g * P:(g + 1) * P], ot[:, g, t * P:(t + 1) * P], ident[:])
                    last.then_inc(o_turned, 1)

            def turn_back(c, later):
                if later:
                    pe.wait_ge(ln.xl_ready, c * KC - KC)
                for ch in range(KC):
                    for t in range(TPC):
                        if ch == 0:
                            pe.wait_ge(on_ready, c * TPC + t + 1)
                        last = pe.transpose(banks["T"][ch][:, t * P:(t + 1) * P], on[:, t, ch * P:(ch + 1) * P], ident[:])
                    last.then_inc(ot_ready, 1)

            def project_out(c, nxt):
                pe.wait_ge(ol_ready, c * KC + KC)
                if nxt:
                    pe.wait_ge(on_ready, c * TPC + 2 * TPC)
                cols = slice(W_OUT, W_OUT + E)
                for t in range(TPC):
                    toks = slice(t * P, (t + 1) * P)
                    project(pe, o_bank[t // 2][:, (t % 2) * E:(t % 2 + 1) * E],
                            [oh[:, ch, toks] for ch in range(KC)], [ol[:, ch, toks] for ch in range(KC)],
                            [wh[:, ch, cols] for ch in range(KC)],
                            [wl[:, ch, cols] for ch in range(KC)]).then_inc(op_ready, 1)

            def step(c, prev, nxt, prev_first=False):
                k = FIRST if prev_first else c - 1
                turn_back(c, prev and not prev_first)
                if nxt:
                    turn(c + 1, first=not prev)
                if prev:
                    pe.wait_ge(ol_ready, c * KC + KC)
                    ln.pe_transpose(pe, k, ident)
                project_out(c, nxt)
                if prev:
                    for t in range(TPC):
                        ffn.pe_tile(pe, k, t)

            turn(0, first=True)
            step(0, False, True)
            step(1, True, True, True)
            with pe.Fori(2, NCHUNK - 1) as c:
                step(c, True, True)
            step(NCHUNK - 1, True, False)
            ln.pe_transpose(pe, NCHUNK - 1, ident)
            for t in range(TPC):
                ffn.pe_tile(pe, NCHUNK - 1, t)


def macaron(nc, x, wqkv_t, wsh_t, wex_t, wgate, wout_t, bias, out):
    scr_qk = nc.dram_tensor("scr_qk", [B, 2, 2, E, T // CHUNK, CHUNK], F32).ap()
    scr_v = nc.dram_tensor("scr_v", [NCHUNK, TPC, P, E], F32).ap()
    scr_x1 = nc.dram_tensor("scr_x1", [NCHUNK, P, TPC, E], F32).ap()
    scr_o = nc.dram_tensor("scr_o", [NG, P, 2, CHUNK], F32).ap()
    scratch = {
        "qk": scr_qk,
        "qk_b": scr_qk.rearrange("b k q (g h d) f n -> b k q g h d (f n)", g=GPB, h=GH),
        "v": scr_v,
        "v_b": scr_v.rearrange("(b f) t p (g n) -> b (f t) p g n", f=2, g=GPB),
        "x1": scr_x1,
        "o": scr_o,
        "o_b": scr_o.rearrange("(b g) r f n -> b g r f n", g=GPB),
    }
    io = {
        "x": x.rearrange("(c t p) e -> c p t e", t=TPC, p=P),
        "out": out.rearrange("(c t p) e -> c p t e", t=TPC, p=P),
        "weights": [(wqkv_t, W_QK), (wsh_t, W_SH), (wex_t, W_EX), (wgate, W_EX + E), (wout_t, W_OUT)],
        "bias": bias,
    }
    with ExitStack() as ctx:
        ar = Arena(nc, ctx)
        psum = [ctx.enter_context(nc.psum_tensor(f"bank{n}", [P, BANK], F32)) for n in range(8)]
        ident = ar.sb("ident", [P, P])
        mhalf = ar.sb("mhalf", [P, TPC])
        zero = ar.sb("zero", [P, TPC])
        hbias = ar.sb("hbias", [P, E])
        wh = ar.sb("wh", [P, KC, WCOLS], F32R)
        wl = ar.sb("wl", [P, KC, WCOLS], F32R)
        const = (ident, mhalf, zero, hbias, wh, wl, Hold(ar))
        stage_a(nc, psum, const, io, scratch)
        stage_b(nc, psum, const, scratch)
        stage_c(nc, psum, const, io, scratch)


def kernel(**inputs):
    import numpy as np
    import concourse.bacc as bacc
    from concourse.bass_utils import run_bass_kernel_spmd

    x = np.asarray(inputs["L0_attn_query"])
    arrays = {
        "x": np.ascontiguousarray(x.reshape(B * T, E)),
        "wqkv_t": np.ascontiguousarray(np.asarray(inputs["L0_attn_in_proj_weight"]).T),
        "wsh_t": np.ascontiguousarray(np.asarray(inputs["L0_ffn_W_shared"]).T),
        "wex_t": np.ascontiguousarray(np.asarray(inputs["L0_ffn_W_expert"]).T),
        "wgate": np.ascontiguousarray(np.asarray(inputs["L0_ffn_W_gate"])),
        "wout_t": np.ascontiguousarray(np.asarray(inputs["L0_attn_out_proj_weight"]).T),
        "bias": np.ascontiguousarray(np.asarray(inputs["L0_ffn_bias"])),
    }
    nc = bacc.Bacc("TRN2", target_bir_lowering=False, num_devices=1)
    nc.disable_value_cache = True
    args = [nc.dram_tensor(n, a.shape, mybir.dt.from_np(a.dtype), kind="ExternalInput").ap() for n, a in arrays.items()]
    out = nc.dram_tensor("out", [B * T, E], F32, kind="ExternalOutput").ap()
    macaron(nc, *args, out)
    got = run_bass_kernel_spmd(nc, [arrays], core_ids=[0])
    return got.results[0]["out"].reshape(B, T, E)
```

```python
from contextlib import ExitStack

import concourse.bass as bass
from concourse import mybir

F32 = mybir.dt.float32
F32R = mybir.dt.float32r
BF16 = mybir.dt.bfloat16
ALU = mybir.AluOpType
ACT = mybir.ActivationFunctionType
AX = mybir.AxisListType

P = 128
B, T, E = 8, 1024, 256
H, D = 16, 16
NEXP = 7
EPS = 1e-5
CHUNK = 512
TPC = CHUNK // P
NCHUNK = B * T // CHUNK
KC = E // P
GH = 4
NG = B * H // GH
GPB = H // GH
KT = T // P
BANK = 512
YL = E + NEXP + 1

W_QK, W_V, W_SH, W_EX, W_OUT = 0, 2 * E, 3 * E, 4 * E, 4 * E + YL
WCOLS = W_OUT + E

SROWS = 4 * D
SROWS_M = SROWS + 2
NBUF = 3
AHEAD = 3
MASKED = -1.0e38

SLOTS = [
    [(0, 0, 512, 0)],
    [(0, 512, 512, 0)],
    [(1, 128, 384, 0), (7, 896, 128, 384)],
    [(2, 256, 256, 0), (6, 768, 256, 256)],
    [(3, 384, 128, 0), (5, 640, 384, 128)],
    [(1, 512, 512, 0)],
    [(2, 512, 512, 0)],
    [(3, 512, 512, 0)],
    [(4, 512, 512, 0)],
]
NSLOT = len(SLOTS)
TILES = NSLOT * GH
DIAG = [[off for j, q0, n, off in s if q0 == j * P] for s in SLOTS]
DIAG_SLOTS = [s for s in range(NSLOT) if DIAG[s]]
LOW_DONE, HIGH_DONE = 4, 8

MAX_SLOTS = [
    [(3, 0, 512, 0)],
    [(7, 512, 512, 0)],
    [(7, 0, 512, 0)],
    [(6, 0, 512, 0)],
    [(5, 0, 512, 0)],
    [(4, 0, 512, 0)],
    [(2, 0, 384, 0), (0, 0, 128, 384)],
    [(6, 512, 384, 0), (4, 512, 128, 384)],
    [(1, 0, 256, 0), (5, 512, 256, 256)],
]
EARLY = (B - 1) * H
SB = 3
M_BANK = 1


class Arena:

    def __init__(self, nc, ctx, hold=None):
        self.nc, self.ctx, self.hold = nc, ctx, hold

    def sb(self, name, shape, dt=F32):
        return self.ctx.enter_context(self.nc.sbuf_tensor(name, shape, dt))

    def sem(self, name):
        return self.ctx.enter_context(self.nc.semaphore(name))


class Chain:

    def __init__(self, eng, sem, base):
        self.eng, self.sem, self.base, self.n = eng, sem, base, 0

    def __call__(self, ins):
        ins.then_inc(self.sem, 1)
        self.n += 1
        self.eng.wait_ge(self.sem, self.base + self.n)


class Hold:

    COLS = 8

    def __init__(self, ar):
        self.dve_out = ar.sb("hold_dve", [P, self.COLS])
        self.pool_out = ar.sb("hold_pool", [P, self.COLS])

    def dve(self, dve, col):
        dve.memset(self.dve_out[:, col:col + 1], 0.0)

    def pool(self, pool, col, zero):
        pool.tensor_tensor(self.pool_out[:, col:col + 1], zero[:, 0:1], zero[:, 1:2], ALU.add)


def project(pe, out, lh, ll, rh, rl):
    terms = [(a[ch], b[ch]) for ch in range(KC) for a, b in ((lh, rh), (lh, rl), (ll, rh))]
    for n, (a, b) in enumerate(terms):
        last = pe.matmul(out, a, b, start=(n == 0), stop=(n == len(terms) - 1))
    return last


GATE_LINKS = 10


class Ffn:

    def __init__(self, ar, name, w, banks, zero, col=0):
        self.w, self.banks, self.hold = w, banks, ar.hold
        sb, sem = (lambda n, s, d=F32: ar.sb(f"{name}_{n}", s, d)), (lambda n: ar.sem(f"{name}_{n}"))
        self.stats = sb("stats", [P, TPC, 6])
        self.mv = sb("mv", [P, TPC, 2])
        self.veps = sb("veps", [P, TPC])
        self.nmean = sb("nmean", [P, TPC])
        self.zero, self.col = zero, col
        self.rstd = sb("rstd", [P, TPC])
        self.nbias = sb("nbias", [P, TPC])
        self.xn = sb("xn", [P, TPC, E])
        self.xh = sb("xh", [P, KC, CHUNK], F32R)
        self.xl = sb("xl", [P, KC, CHUNK], F32R)
        self.bn_done = sem("bn_done")
        self.mv_ready = sem("mv_ready")
        self.pool_chain = sem("pool_chain")
        self.xn_ready = sem("xn_ready")
        self.t_ready = sem("t_ready")
        self.xh_ready = sem("xh_ready")
        self.xl_ready = sem("xl_ready")

    def dve_stats(self, dve, k, t, x):
        dve.bn_stats(self.stats[:, t, :], x[:, t, :]).then_inc(self.bn_done, 1)

    def dve_aggregate(self, dve, k, first=False):
        dve.wait_ge(self.bn_done, k * TPC + TPC)
        if not first:
            dve.wait_ge(self.xn_ready, k * TPC)
        self.hold.dve(dve, self.col)
        for t in range(TPC):
            dve.bn_aggr(self.mv[:, t, :], self.stats[:, t, :]).then_inc(self.mv_ready, 1)

    def pool_rstd(self, pool, k, mhalf, first=False):
        ch = Chain(pool, self.pool_chain, k * 4)
        pool.wait_ge(self.mv_ready, k * TPC + TPC)
        if not first:
            pool.wait_ge(self.xn_ready, k * TPC)
        pool.tensor_tensor(self.nmean[:], self.zero[:], self.mv[:, :, 0], ALU.subtract).then_inc(self.pool_chain, 1)
        ch.n += 1
        ch(pool.tensor_scalar(self.veps[:], self.mv[:, :, 1], EPS, None, ALU.add))
        ch(pool.tensor_tensor(self.rstd[:], self.veps[:], mhalf[:], ALU.pow))
        pool.tensor_tensor(self.nbias[:], self.nmean[:], self.rstd[:], ALU.mult).then_inc(self.pool_chain, 1)

    def act_normalise(self, act, k, x, first=False, tiles=range(TPC)):
        if tiles[0] == 0:
            act.wait_ge(self.pool_chain, k * 4 + 4)
            if not first:
                act.wait_ge(self.t_ready, k * KC)
        for t in tiles:
            act.activation(self.xn[:, t, :], x[:, t, :], ACT.Identity, scale=self.rstd[:, t:t + 1],
                           bias=self.nbias[:, t:t + 1]).then_inc(self.xn_ready, 1)

    def pe_transpose(self, pe, k, ident, src=None):
        src = self.xn if src is None else src
        for ch in range(KC):
            for t in range(TPC):
                if ch == 0:
                    pe.wait_ge(self.xn_ready, k * TPC + t + 1)
                last = pe.transpose(self.banks["T"][ch][:, t * P:(t + 1) * P],
                                    src[:, t, ch * P:(ch + 1) * P], ident[:])
            last.then_inc(self.t_ready, 1)

    def act_high(self, act, k):
        for ch in range(KC):
            act.wait_ge(self.t_ready, k * KC + ch + 1)
            act.copy(self.xh[:, ch, :], self.banks["T"][ch][:]).then_inc(self.xh_ready, 1)

    def dve_low(self, dve, k):
        for ch in range(KC):
            dve.wait_ge(self.xh_ready, k * KC + ch + 1)
            dve.tensor_tensor(self.xl[:, ch, :], self.banks["T"][ch][:], self.xh[:, ch, :].bitcast(F32),
                              ALU.subtract).then_inc(self.xl_ready, 1)

    def tile(self, t):
        cols = slice(t * P, (t + 1) * P)
        return [self.xh[:, ch, cols] for ch in range(KC)], [self.xl[:, ch, cols] for ch in range(KC)]

    def whole(self):
        return [self.xh[:, ch, :] for ch in range(KC)], [self.xl[:, ch, :] for ch in range(KC)]


class Experts:

    def __init__(self, ar, name, w, banks, ln):
        self.w, self.banks, self.ln = w, banks, ln
        sb, sem = (lambda n, s, d=F32: ar.sb(f"{name}_{n}", s, d)), (lambda n: ar.sem(f"{name}_{n}"))
        self.xb = sb("xb", [P, TPC, E])
        self.acc = sb("acc", [P, TPC, E])
        self.yl = sb("yl", [P, TPC, YL])
        self.lmax = sb("lmax", [P, TPC])
        self.dl = sb("dl", [P, TPC, NEXP])
        self.ex = sb("ex", [P, TPC, 8])
        self.top = sb("top", [P, TPC, 8])
        self.den = sb("den", [P, TPC])
        self.rden = sb("rden", [P, TPC])
        self.w2 = sb("w2", [P, TPC, 2])
        self.wsum = sb("wsum", [P, TPC])
        self.ffn_ready = sem("ffn_ready")
        self.yl_ready = sem("yl_ready")
        self.acc_ready = sem("acc_ready")
        self.xb_ready = sem("xb_ready")
        self.gate_chain = sem("gate_chain")
        self.ex_ready = sem("ex_ready")
        self.out_ready = sem("out_ready")

    def pe_tile(self, pe, k, t):
        n = k * TPC + t
        sh, ex = self.banks["F"][t % 2]
        if t == 0:
            pe.wait_ge(self.ln.xl_ready, k * KC + KC)
        if not (k is FIRST and t < 2):
            pe.wait_ge(self.yl_ready, n - 1)
            pe.wait_ge(self.acc_ready, n - 1)
        lh, ll = self.ln.tile(t)
        wh, wl = self.w
        cols = slice(W_EX, W_EX + YL)
        project(pe, ex[:, 0:YL], lh, ll, [wh[:, ch, cols] for ch in range(KC)], [wl[:, ch, cols] for ch in range(KC)])
        cols = slice(W_SH, W_SH + E)
        project(pe, sh[:, 0:E], lh, ll, [wh[:, ch, cols] for ch in range(KC)],
                [wl[:, ch, cols] for ch in range(KC)]).then_inc(self.ffn_ready, 1)

    def act_tile(self, act, k, t, first=False):
        act.wait_ge(self.ffn_ready, k * TPC + t + 1)
        if not first:
            act.wait_ge(self.out_ready, k * TPC - TPC + t + 1)
        act.mul(self.yl[:, t, :], self.banks["F"][t % 2][1][:, 0:YL], 0.5).then_inc(self.yl_ready, 1)

    def dve_tile(self, dve, k, t):
        dve.wait_ge(self.ffn_ready, k * TPC + t + 1)
        dve.wait_ge(self.xb_ready, k * TPC + t + 1)
        dve.scalar_tensor_tensor(out=self.acc[:, t, :], in0=self.banks["F"][t % 2][0][:, 0:E], scalar=0.5,
                                 in1=self.xb[:, t, :], op0=ALU.mult, op1=ALU.add).then_inc(self.acc_ready, 1)

    def dve_logits(self, dve, k):
        ch = Chain(dve, self.gate_chain, k * GATE_LINKS)
        dve.wait_ge(self.yl_ready, k * TPC + TPC)
        logits = self.yl[:, :, E:E + NEXP]
        ch(dve.tensor_reduce(self.lmax[:], logits, AX.X, ALU.max))
        ch(dve.tensor_tensor(self.dl[:], logits, self.lmax[:].unsqueeze(2).to_broadcast([P, TPC, NEXP]), ALU.subtract))

    def dve_gate(self, dve, k):
        ch = Chain(dve, self.gate_chain, k * GATE_LINKS)
        ch.n = 2
        dve.wait_ge(self.ex_ready, k + 1)
        self.ln.hold.dve(dve, 2)
        for t in range(TPC):
            last = dve.max(self.top[:, t, :], self.ex[:, t, :])
            if t < TPC - 1:
                last.then_inc(self.gate_chain, 1)
                ch.n += 1
        ch(last)
        ch(dve.tensor_tensor(self.den[:], self.top[:, :, 0], self.top[:, :, 1], ALU.add))
        ch(dve.reciprocal(self.rden[:], self.den[:]))
        ch(dve.tensor_tensor(self.w2[:], self.top[:, :, 0:2], self.rden[:].unsqueeze(2).to_broadcast([P, TPC, 2]), ALU.mult))
        ch(dve.tensor_tensor(self.wsum[:], self.w2[:, :, 0], self.w2[:, :, 1], ALU.add))
        assert ch.n == GATE_LINKS

    def act_exp(self, act, k):
        act.wait_ge(self.gate_chain, k * GATE_LINKS + 2)
        act.activation(self.ex[:, :, 0:NEXP], self.dl[:], ACT.Exp, scale=2.0).then_inc(self.ex_ready, 1)

    def dve_out(self, dve, k, t, out):
        if t == 0:
            dve.wait_ge(self.acc_ready, k * TPC + TPC)
        dve.scalar_tensor_tensor(out=out[:, t, :], in0=self.yl[:, t, 0:E], scalar=self.wsum[:, t:t + 1],
                                 in1=self.acc[:, t, :], op0=ALU.mult, op1=ALU.add).then_inc(self.out_ready, 1)

    def pool_xb(self, pool, k, x, hbias, first=False):
        for t in range(TPC):
            if not first:
                pool.wait_ge(self.acc_ready, k * TPC - TPC + t + 1)
            pool.tensor_tensor(self.xb[:, t, :], x[:, t, :], hbias[:], ALU.add).then_inc(self.xb_ready, 1)


class _First(int):
    pass


FIRST = _First(0)


def stage_a(nc, psum, const, io, scratch):
    ident, mhalf, zero, hbias, wh, wl, hold = const
    with ExitStack() as ctx:
        ar = Arena(nc, ctx, hold)
        banks = {"T": psum[0:2], "F": [psum[2:4], psum[4:6]], "Q": psum[6:8]}
        x = ar.sb("a_x", [P, TPC, E])
        x1 = ar.sb("a_x1", [P, TPC, E])
        qk = ar.sb("a_qk", [P, 2 * KC, 2, CHUNK], F32R)
        v = ar.sb("a_v", [P, TPC, E])
        stage = ar.sb("a_stage", [P, KC, WCOLS])
        brow = ar.sb("a_brow", [P, E])
        ln1 = Ffn(ar, "a_ln1", (wh, wl), banks, zero)
        ln2 = Ffn(ar, "a_ln2", (wh, wl), banks, zero, 1)
        ffn = Experts(ar, "a_ffn", (wh, wl), banks, ln1)
        w_loaded = ar.sem("w_loaded")
        pad_ready = ar.sem("pad_ready")
        w_ready = ar.sem("w_ready")
        b_ready = ar.sem("b_ready")
        c_ready = ar.sem("c_ready")
        x_loaded = ar.sem("x_loaded")
        x1_stored = ar.sem("x1_stored")
        qk_stored = ar.sem("qk_stored")
        v_stored = ar.sem("v_stored")
        qkv_ready = ar.sem("qkv_ready")
        qh_ready = ar.sem("qh_ready")
        ql_ready = ar.sem("ql_ready")
        NQK, QKV = 2 * KC, 2 * KC + TPC // 2
        PROJ = [("qk", 0), ("qk", 1), ("v", 0), ("v", 1), ("qk", 2), ("qk", 3)]
        PROJ_EARLY = 3
        proj_bank = [*banks["F"][0], *banks["F"][1], *banks["Q"]]

        block = ctx.enter_context(nc.Block())

        @block.sync
        def _(sp):
            for src, col in io["weights"]:
                n = src.shape[1]
                sp.dma_start(stage[:, :, col:col + n], src.rearrange("(k p) n -> p k n", p=P)).then_inc(w_loaded, 16)
            sp.dma_start(brow[:], io["bias"].rearrange("(a n) -> a n", a=1).to_broadcast([P, E])).then_inc(w_loaded, 16)

            def load(c):
                sp.dma_start(x[:], io["x"][bass.ds(c, 1)].rearrange("a p t e -> p (a t) e")).then_inc(x_loaded, 16)

            def store_x1(c):
                sp.wait_ge(ffn.out_ready, c * TPC + TPC)
                sp.dma_start(scratch["x1"][bass.ds(c, 1)].rearrange("a p t e -> p (a t) e"), x1[:]).then_inc(x1_stored, 16)

            def store_qkv(c):
                for j in range(NQK):
                    sp.wait_ge(ql_ready, c * NQK + j + 1)
                    dst = scratch["qk"][bass.ds(c // 2, 1), j // KC, :, (j % KC) * P:(j % KC + 1) * P, bass.ds(c % 2, 1)]
                    sp.dma_start(dst.rearrange("a q r f n -> r (a q) (f n)"), qk[:, j, :, :].bitcast(F32)).then_inc(qk_stored, 16)
                sp.wait_ge(qh_ready, c * QKV + QKV)
                sp.dma_start(scratch["v"][bass.ds(c, 1)].rearrange("a t p e -> p (a t) e"), v[:]).then_inc(v_stored, 16)

            def step(c, prev, nxt2):
                if nxt2:
                    sp.wait_ge(ln1.xn_ready, c * TPC + 2 * TPC)
                    sp.wait_ge(ffn.xb_ready, c * TPC + 2 * TPC)
                    load(c + 2)
                store_x1(c)
                if prev:
                    store_qkv(c - 1)

            load(0)
            sp.wait_ge(ln1.xn_ready, TPC)
            sp.wait_ge(ffn.xb_ready, TPC)
            load(1)
            step(0, False, True)
            with sp.Fori(1, NCHUNK - 2) as c:
                step(c, True, True)
            step(NCHUNK - 2, True, False)
            step(NCHUNK - 1, True, False)
            store_qkv(NCHUNK - 1)
            sp.wait_ge(x1_stored, NCHUNK * 16)
            sp.wait_ge(qk_stored, NCHUNK * NQK * 16)
            sp.wait_ge(v_stored, NCHUNK * 16)

        @block.gpsimd
        def _(pool):
            pool.memset(ident[:], 0.0).then_inc(c_ready, 1)
            pool.memset(mhalf[:], -0.5).then_inc(c_ready, 1)
            pool.memset(zero[:], 0.0).then_inc(c_ready, 1)
            pool.memset(ffn.ex[:], 0.0).then_inc(c_ready, 1)
            pool.memset(stage[:, :, W_EX + E + NEXP:W_EX + YL], 0.0).then_inc(pad_ready, 1)
            pool.wait_ge(c_ready, 4)
            pool.affine_select(out=ident[:], in_=ident[:], compare_op=ALU.not_equal, fill=1.0, base=0,
                               pattern=[[-1, P]], channel_multiplier=1).then_inc(c_ready, 1)
            pool.wait_ge(x_loaded, 16)
            pool.wait_ge(b_ready, 1)
            ln1.pool_rstd(pool, 0, mhalf, first=True)
            ffn.pool_xb(pool, 0, x, hbias, first=True)

            def step(c, nxt):
                if nxt:
                    ln1.pool_rstd(pool, c + 1, mhalf)
                    ffn.pool_xb(pool, c + 1, x, hbias)
                ln2.pool_rstd(pool, c, mhalf, first=(c is FIRST))

            step(FIRST, True)
            with pool.Fori(1, NCHUNK - 1) as c:
                step(c, True)
            step(NCHUNK - 1, False)

        @block.scalar
        def _(act):
            act.preload_act_table(ACT.Exp)
            act.wait_ge(x_loaded, 16)
            ln1.act_normalise(act, 0, x, first=True)
            ln1.act_high(act, 0)

            def high(c, j, first):
                kind, i = PROJ[j]
                act.wait_ge(qkv_ready, c * QKV + j + 1)
                if kind == "v":
                    if not first:
                        act.wait_ge(v_stored, c * 16)
                    act.copy(v[:, 2 * i:2 * i + 2, :], proj_bank[j][:].rearrange("p (t e) -> p t e", t=2)).then_inc(qh_ready, 1)
                else:
                    if not first:
                        act.wait_ge(qk_stored, c * NQK * 16)
                    act.mul(qk[:, i, 0, :], proj_bank[j][:], 0.25 if i < KC else 1.0).then_inc(qh_ready, 1)

            def step(c, prev, nxt, prev_first=False):
                first = c is FIRST

                def norm2(*tiles):
                    if prev:
                        ln2.act_normalise(act, FIRST if prev_first else c - 1, x1, prev_first, tiles)

                def norm1(*tiles):
                    if nxt:
                        ln1.act_normalise(act, c + 1, x, False, tiles)

                norm2(0)
                ffn.act_tile(act, c, 0, first)
                norm2(1, 2)
                ffn.act_tile(act, c, 1, first)
                norm2(3)
                ffn.act_tile(act, c, 2, first)
                if prev:
                    ln2.act_high(act, c - 1)
                norm1(0)
                ffn.act_tile(act, c, 3, first)
                norm1(1)
                ffn.act_exp(act, c)
                norm1(2, 3)
                if prev:
                    for j in range(PROJ_EARLY):
                        high(c - 1, j, prev_first)
                if nxt:
                    ln1.act_high(act, c + 1)
                if prev:
                    for j in range(PROJ_EARLY, QKV):
                        high(c - 1, j, prev_first)

            step(FIRST, False, True)
            step(1, True, True, True)
            with act.Fori(2, NCHUNK - 1) as c:
                step(c, True, True)
            step(NCHUNK - 1, True, False)
            ln2.act_normalise(act, NCHUNK - 1, x1)
            ln2.act_high(act, NCHUNK - 1)
            for j in range(QKV):
                high(NCHUNK - 1, j, False)

        @block.vector
        def _(dve):
            dve.wait_ge(w_loaded, 16 * (len(io["weights"]) + 1))
            dve.wait_ge(pad_ready, 1)
            dve.tensor_scalar(hbias[:], brow[:], 0.5, None, ALU.mult).then_inc(b_ready, 1)
            dve.tensor_copy(wh[:], stage[:]).then_inc(w_ready, 1)
            dve.wait_ge(w_ready, 1)
            dve.tensor_tensor(wl[:], stage[:], wh[:].bitcast(F32), ALU.subtract).then_inc(w_ready, 1)

            def low(c, i):
                j = PROJ.index(("qk", i))
                dve.wait_ge(qh_ready, c * QKV + j + 1)
                dve.scalar_tensor_tensor(out=qk[:, i, 1, :], in0=proj_bank[j][:], scalar=0.25 if i < KC else 1.0,
                                         in1=qk[:, i, 0, :].bitcast(F32), op0=ALU.mult,
                                         op1=ALU.subtract).then_inc(ql_ready, 1)

            def step(c, prev, nxt):
                ffn.dve_tile(dve, c, 0)
                if nxt:
                    dve.wait_ge(x_loaded, c * 16 + 32)
                    for t in (0, 1):
                        ln1.dve_stats(dve, c + 1, t, x)
                ffn.dve_tile(dve, c, 1)
                if nxt:
                    for t in (2, 3):
                        ln1.dve_stats(dve, c + 1, t, x)
                    ln1.dve_aggregate(dve, c + 1)
                ffn.dve_tile(dve, c, 2)
                if prev:
                    ln2.dve_low(dve, c - 1)
                ffn.dve_tile(dve, c, 3)
                ffn.dve_logits(dve, c)
                ffn.dve_gate(dve, c)
                if prev:
                    low(c - 1, 0)
                    dve.wait_ge(x1_stored, c * 16)
                    dve.wait_ge(ln2.xn_ready, c * TPC)
                for t in range(TPC):
                    ffn.dve_out(dve, c, t, x1)
                    if t:
                        dve.wait_ge(ffn.out_ready, c * TPC + t)
                        ln2.dve_stats(dve, c, t - 1, x1)
                dve.wait_ge(ffn.out_ready, c * TPC + TPC)
                ln2.dve_stats(dve, c, TPC - 1, x1)
                ln2.dve_aggregate(dve, c, first=(c is FIRST))
                if prev:
                    low(c - 1, 1)
                if nxt:
                    ln1.dve_low(dve, c + 1)
                if prev:
                    low(c - 1, 2)
                    low(c - 1, 3)

            dve.wait_ge(x_loaded, 16)
            for t in range(TPC):
                ln1.dve_stats(dve, 0, t, x)
            ln1.dve_aggregate(dve, 0, first=True)
            ln1.dve_low(dve, 0)
            step(FIRST, False, True)
            with dve.Fori(1, NCHUNK - 1) as c:
                step(c, True, True)
            step(NCHUNK - 1, True, False)
            ln2.dve_low(dve, NCHUNK - 1)
            for i in range(NQK):
                low(NCHUNK - 1, i)

        @block.tensor
        def _(pe):
            def qkv(c, js, first=False, last=False):
                th, tl = ln2.whole()
                for j in js:
                    kind, i = PROJ[j]
                    if j == 0:
                        pe.wait_ge(ln2.xl_ready, c * KC + KC)
                    if last:
                        pe.wait_ge(ql_ready, c * NQK)
                        pe.wait_ge(qh_ready, c * QKV)
                    elif j in (0, 2):
                        pe.wait_ge(ffn.yl_ready, c * TPC + TPC + 3 + j // 2)
                        pe.wait_ge(ffn.acc_ready, c * TPC + TPC + 3 + j // 2)
                    elif j == 4 and not first:
                        pe.wait_ge(ql_ready, c * NQK)
                    bank = proj_bank[j]
                    if kind == "qk":
                        cols = slice(W_QK + i * P, W_QK + (i + 1) * P)
                        project(pe, bank[:], [wh[:, ch, cols] for ch in range(KC)], [wl[:, ch, cols] for ch in range(KC)],
                                th, tl).then_inc(qkv_ready, 1)
                    else:
                        cols = slice(W_V, W_V + E)
                        for t in (2 * i, 2 * i + 1):
                            lh, ll = ln2.tile(t)
                            done = project(pe, bank[:, (t % 2) * E:(t % 2 + 1) * E], lh, ll,
                                           [wh[:, ch, cols] for ch in range(KC)], [wl[:, ch, cols] for ch in range(KC)])
                        done.then_inc(qkv_ready, 1)

            def step(c, prev, nxt, prev_first=False):
                if prev and not prev_first:
                    pe.wait_ge(ql_ready, c * NQK - 2 * NQK + 2)
                ffn.pe_tile(pe, c, 0)
                if prev and not prev_first:
                    pe.wait_ge(qh_ready, c * QKV - 2 * QKV + 4)
                ffn.pe_tile(pe, c, 1)
                ffn.pe_tile(pe, c, 2)
                if prev:
                    ln2.pe_transpose(pe, c - 1, ident)
                ffn.pe_tile(pe, c, 3)
                if prev:
                    qkv(c - 1, range(PROJ_EARLY), prev_first)
                if nxt:
                    ln1.pe_transpose(pe, c + 1, ident)
                if prev:
                    qkv(c - 1, range(PROJ_EARLY, QKV), prev_first)

            pe.wait_ge(c_ready, 5)
            pe.wait_ge(w_ready, 2)
            ln1.pe_transpose(pe, 0, ident)
            step(FIRST, False, True)
            step(1, True, True, True)
            with pe.Fori(2, NCHUNK - 1) as c:
                step(c, True, True)
            step(NCHUNK - 1, True, False)
            ln2.pe_transpose(pe, NCHUNK - 1, ident)
            qkv(NCHUNK - 1, range(QKV), last=True)


def stage_b(nc, psum, const, scratch):
    ident, _, zero, *_, hold = const
    with ExitStack() as ctx:
        ar = Arena(nc, ctx, hold)
        s_bank, m_bank, o_bank = psum[0:SB], psum[SB:2 * SB], psum[2 * SB:2 * SB + 2]
        qs = [ar.sb(f"b_qs{n}", [P, GH, T], F32R) for n in range(NBUF)]
        ks = [ar.sb(f"b_ks{n}", [P, GH, T], F32R) for n in range(NBUF)]
        vx = [ar.sb(f"b_vx{n}", [P, KT, GH, 2 * D]) for n in range(NBUF)]
        vin = ar.sb("b_vin", [P, KT, GH * D])
        probs = ar.sb("b_probs", [P, NBUF, GH, BANK])
        o = ar.sb("b_o", [P, 2, BANK])
        mask = ar.sb("b_mask", [P, BANK])
        junk = ar.sb("b_junk", [P, SB, BANK], BF16)
        rest = ar.sb("b_rest", [P, T])
        pm = ar.sb("b_pm", [P, 2, GH, KT])
        mparts = ar.sb("b_mparts", [P, P // (GH * KT), GH * KT], F32R)
        mt = ar.sb("b_mt", [2 * GH * KT, P], F32R)
        den = ar.sb("b_den", [EARLY, T])

        c_ready = ar.sem("b_c_ready")
        z_ready = ar.sem("b_z_ready")
        qz_ready = ar.sem("b_qz_ready")
        kz_ready = ar.sem("b_kz_ready")
        stacked = [ar.sem(f"b_stacked{n}") for n in range(NBUF)]
        v_loaded = ar.sem("b_v_loaded")
        vx_ready = ar.sem("b_vx_ready")
        m_tile = ar.sem("b_m_tile")
        m_read = ar.sem("b_m_read")
        m_chain = ar.sem("b_m_chain")
        m_turned = ar.sem("b_m_turned")
        m_out = ar.sem("b_m_out")
        m_placed = [ar.sem(f"b_m_placed{n}") for n in range(NBUF)]
        s_tile = ar.sem("b_s_tile")
        p_ready = ar.sem("b_p_ready")
        p_masked = ar.sem("b_p_masked")
        pv_done = ar.sem("b_pv_done")
        o_out = ar.sem("b_o_out")
        o_stored = [ar.sem(f"b_o_stored{n}") for n in range(2)]
        den_loaded = ar.sem("b_den_loaded")
        r_ready = ar.sem("b_r_ready")
        r_stored = ar.sem("b_r_stored")
        STACK = 16 * 8
        ND = len(DIAG_SLOTS)

        class Group:

            def __init__(self, r, k):
                if isinstance(r, int):
                    r, k = 0, NBUF * r + k
                self.r, self.k, self.buf = r, k, k % NBUF

            def at(self, per, more=0):
                return self.r * (NBUF * per) + (self.k * per + more)

            def turn(self, per, more=0):
                return self.r * per + (self.k // NBUF * per + more)

            def next(self, n):
                return Group(self.r, self.k + n) if not isinstance(self.r, int) else Group(0, self.k + n)

            @property
            def first(self):
                return isinstance(self.r, int) and self.k == 0

        def groups(eng, step):
            step(Group(0, 0), False)
            with eng.Fori(0, (NG - 2) // NBUF) as r:
                for k in range(1, NBUF + 1):
                    step(Group(r, k), False)
            step(Group(0, NG - 1), True)

        assert (NG - 2) % NBUF == 0
        block = ctx.enter_context(nc.Block())

        @block.sync
        def _(sp):
            def load(g):
                i = g.at(1) % NG
                b, gg = i // GPB, i % GPB
                for kind, dst, order in ((0, qs[g.buf], (0, 0, 1, 1)), (1, ks[g.buf], (0, 1, 0, 1))):
                    for n, part in enumerate(order):
                        src = scratch["qk_b"][bass.ds(b, 1), kind, part, bass.ds(gg, 1)]
                        sp.dma_start(dst[n * D:(n + 1) * D, :, :].bitcast(F32),
                                     src.rearrange("a g h d n -> d (a g h) n")).then_inc(stacked[g.buf], 16)

            def load_v(g):
                i = g.at(1)
                b, gg = i // GPB, i % GPB
                sp.dma_start(vin[:], scratch["v_b"][bass.ds(b, 1), :, :, bass.ds(gg, 1)].rearrange(
                    "a k p g n -> p (a k) (g n)")).then_inc(v_loaded, 16)

            def place_m(g):
                sp.wait_ge(m_out, g.at(1, 1))
                sp.dma_start(qs[g.buf][SROWS:SROWS_M, :, :].rearrange("r h (i p) -> r (h i) p", p=P).bitcast(F32),
                             mt[:].bitcast(F32)).then_inc(m_placed[g.buf], 16)

            def store(g, half):
                sp.wait_ge(o_out, g.at(2, half + 1))
                sp.dma_start(scratch["o"][bass.ds(g.at(1), 1), :, half].rearrange("a r n -> (a r) n"),
                             o[:, half, :]).then_inc(o_stored[half], 16)

            load(Group(0, 0))
            load(Group(0, 1))
            load_v(Group(0, 0))
            sp.wait_ge(qz_ready, NBUF)
            place_m(Group(0, 0))

            def step(g, last):
                if not last:
                    if not g.first:
                        sp.wait_ge(s_tile, g.at(TILES))
                    load(g.next(2))
                    sp.wait_ge(vx_ready, g.at(1, 1))
                    load_v(g.next(1))
                if not g.first:
                    store(g.next(-1), 1)
                if not last:
                    place_m(g.next(1))
                else:
                    for half in range(2):
                        sp.wait_ge(o_stored[half], 16 * (NG - GPB))
                    sp.dma_start(den[:], scratch["o_rows"][0:EARLY, D].rearrange("r f n -> r (f n)")).then_inc(den_loaded, 16)
                store(g, 0)

            groups(sp, step)
            sp.wait_ge(r_ready, 1)
            sp.dma_start(scratch["r"][0:EARLY, :], den[:]).then_inc(r_stored, 16)
            store(Group(0, NG - 1), 1)
            for half in range(2):
                sp.wait_ge(o_stored[half], 16 * NG)
            sp.wait_ge(r_stored, 16)

        @block.gpsimd
        def _(pool):
            setup = Chain(pool, c_ready, 0)
            setup(pool.memset(rest[SROWS:P, :], 0.0))
            setup(pool.memset(rest[SROWS:SROWS_M, :], 1.0))
            setup(pool.memset(mask[:], 0.0))
            diag = mask[:, BANK - P:BANK]
            setup(pool.affine_select(out=diag, in_=diag, compare_op=ALU.is_ge, fill=MASKED, base=0,
                                     pattern=[[-1, P]], channel_multiplier=1))
            clear = Chain(pool, qz_ready, 0)
            for n in range(NBUF):
                clear(pool.memset(qs[n][SROWS:P, :, :].bitcast(F32), 0.0))
                setup(pool.memset(vx[n][:], 1.0))

            def expand_v(g):
                pool.wait_ge(v_loaded, g.at(16, 16))
                hold.pool(pool, ND, zero)
                pool.tensor_copy(vx[g.buf][:, :, :, 0:D],
                                 vin[:].rearrange("p k (h d) -> p k h d", h=GH)).then_inc(vx_ready, 1)

            def step(g, last):
                for s in DIAG_SLOTS:
                    pool.wait_ge(p_ready, g.at(TILES, GH * (s + 1)))
                    hold.pool(pool, DIAG_SLOTS.index(s), zero)
                    for n, off in enumerate(DIAG[s]):
                        blk = probs[:, s % NBUF, :, off:off + P]
                        ins = pool.affine_select(out=blk, in_=blk, compare_op=ALU.is_ge, fill=0.0, base=0,
                                                 pattern=[[0, GH], [1, P]], channel_multiplier=-1)
                    ins.then_inc(p_masked, 1)
                    if s == LOW_DONE and not last:
                        expand_v(g.next(1))

            expand_v(Group(0, 0))
            groups(pool, step)

        @block.scalar
        def _(act):
            def out_m(g):
                act.wait_ge(m_turned, g.at(1, 1))
                if not g.first:
                    p = g.next(-1)
                    act.wait_ge(m_placed[p.buf], p.turn(16, 16))
                act.copy(mt[:], m_bank[M_BANK][0:2 * GH * KT, 0:P]).then_inc(m_out, 1)

            def out_o(g, half):
                act.wait_ge(pv_done, g.at(NSLOT, (LOW_DONE, HIGH_DONE)[half] + 1))
                if not g.first:
                    act.wait_ge(o_stored[half], g.at(16))
                act.copy(o[:, half, :], o_bank[half][:]).then_inc(o_out, 1)

            def exp(g, s):
                if not (g.first and s < NBUF):
                    act.wait_ge(pv_done, g.at(NSLOT, s - NBUF + 1))
                for h in range(GH):
                    t = s * GH + h
                    act.wait_ge(s_tile, g.at(TILES, t + 1))
                    act.activation(probs[:, s % NBUF, h, :], s_bank[t % SB][:], ACT.Exp).then_inc(p_ready, 1)

            def step(g, last):
                for s in range(NSLOT):
                    exp(g, s)
                    if s == 2 and not g.first:
                        out_o(g.next(-1), 1)
                    if s == NSLOT - AHEAD and not last:
                        out_m(g.next(1))
                    if s == LOW_DONE + 3:
                        out_o(g, 0)

            act.wait_ge(c_ready, 2)
            for n in range(NBUF):
                for h in range(GH):
                    act.copy(ks[n][SROWS:P, h, :], rest[SROWS:P, :]).then_inc(kz_ready, 1)
            out_m(Group(0, 0))
            groups(act, step)
            out_o(Group(0, NG - 1), 1)

        @block.vector
        def _(dve):
            dve.memset(mparts[:].bitcast(F32), 0.0).then_inc(z_ready, 1)
            dve.wait_ge(z_ready, 1)
            dve.wait_ge(c_ready, 4)

            def maxima(g, a):
                for h in range(GH):
                    t = a * GH + h
                    dve.wait_ge(m_tile, g.at(TILES, t + 1))
                    if not (g.first and t < SB):
                        dve.wait_ge(m_read, g.at(TILES, t - SB + 1))
                    hold.dve(dve, t % 4)
                    bank = m_bank[t % SB]
                    for i, k0, n, off in MAX_SLOTS[a]:
                        src = bank[:, off:off + n]
                        if k0 + n == (i + 1) * P:
                            ins = dve.tensor_tensor_reduce(junk[:, t % SB, off:off + n], src, mask[:, BANK - n:BANK], 1.0, 0.0, ALU.add,
                                                           ALU.max, pm[:, 0, h, i:i + 1])
                        else:
                            ins = dve.tensor_reduce(pm[:, 1, h, i:i + 1], src, AX.X, ALU.max)
                    ins.then_inc(m_read, 1)

            def parts(g):
                ch = Chain(dve, m_chain, g.at(3))
                dve.wait_ge(m_read, g.at(TILES, TILES))
                if not g.first:
                    dve.wait_ge(m_turned, g.at(1))
                two = slice(KT // 2, KT)
                ch(dve.tensor_tensor(pm[:, 0, :, two], pm[:, 0, :, two], pm[:, 1, :, two], ALU.max))
                whole = pm[:, 0, :, :].rearrange("p h i -> p (h i)")
                ch(dve.tensor_scalar(mparts[:, 0, :], whole, -1.0, None, ALU.mult))
                ch(dve.scalar_tensor_tensor(out=mparts[:, 1, :], in0=whole, scalar=-1.0,
                                            in1=mparts[:, 0, :].bitcast(F32), op0=ALU.mult, op1=ALU.subtract))

            def step(g, last):
                if last:
                    dve.wait_ge(den_loaded, 16)
                    dve.reciprocal(den[:], den[:]).then_inc(r_ready, 1)
                    return
                for a in range(AHEAD, NSLOT):
                    maxima(g.next(1), a)
                parts(g.next(1))
                for a in range(AHEAD):
                    maxima(g.next(2), a)

            for a in range(NSLOT):
                maxima(Group(0, 0), a)
            parts(Group(0, 0))
            for a in range(AHEAD):
                maxima(Group(0, 1), a)
            groups(dve, step)

        @block.tensor
        def _(pe):
            def turn_m(g):
                pe.wait_ge(m_chain, g.at(3, 3))
                pe.wait_ge(m_read, g.at(TILES, TILES + M_BANK + 1))
                pe.transpose(m_bank[M_BANK][:, 0:P],
                             mparts[:].rearrange("p q n -> p (q n)").bitcast(F32), ident[:]).then_inc(m_turned, 1)

            def max_tile(g, a, h):
                t = a * GH + h
                if t == 0:
                    pe.wait_ge(stacked[g.buf], g.turn(STACK, STACK))
                if not (g.first and t < SB):
                    pe.wait_ge(m_read, g.at(TILES, t - SB + 1))
                if t == GH and not g.first:
                    pe.wait_ge(m_out, g.at(1))
                for i, k0, n, off in MAX_SLOTS[a]:
                    last = pe.matmul(m_bank[t % SB][:, off:off + n], qs[g.buf][0:SROWS, h, i * P:(i + 1) * P],
                                     ks[g.buf][0:SROWS, h, k0:k0 + n], start=True, stop=True)
                last.then_inc(m_tile, 1)

            def score_tile(g, s, h):
                t = s * GH + h
                if t == 0:
                    pe.wait_ge(m_placed[g.buf], g.turn(16, 16))
                if not (g.first and t < SB):
                    pe.wait_ge(p_ready, g.at(TILES, t - SB + 1))
                for j, q0, n, off in SLOTS[s]:
                    last = pe.matmul(s_bank[t % SB][:, off:off + n], ks[g.buf][:, h, j * P:(j + 1) * P],
                                     qs[g.buf][:, h, q0:q0 + n], start=True, stop=True)
                last.then_inc(s_tile, 1)

            def values(g, s):
                pe.wait_ge(p_ready, g.at(TILES, GH * (s + 1)))
                if DIAG[s]:
                    pe.wait_ge(p_masked, g.at(ND, DIAG_SLOTS.index(s) + 1))
                if s == 0:
                    pe.wait_ge(vx_ready, g.at(1, 1))
                if s < 2 and not g.first:
                    pe.wait_ge(o_out, g.at(2, s - 1))
                for j, q0, n, off in SLOTS[s]:
                    half, col = q0 // BANK, q0 % BANK
                    for h in range(GH):
                        last = pe.matmul(o_bank[half][2 * D * h:2 * D * (h + 1), col:col + n], vx[g.buf][:, j, h, :],
                                         probs[:, s % NBUF, h, off:off + n], start=(j == 0),
                                         stop=(s in (LOW_DONE, HIGH_DONE) and half == (s == HIGH_DONE)),
                                         tile_position=(0, 2 * D * h))
                last.then_inc(pv_done, 1)

            def step(g, last):
                for s in range(NSLOT):
                    for h in range(GH):
                        score_tile(g, s, h)
                        if not last:
                            a = s + AHEAD
                            if a < NSLOT:
                                max_tile(g.next(1), a, h)
                            else:
                                max_tile(g.next(2), a - NSLOT, h)
                    if s == NSLOT - AHEAD and not last:
                        turn_m(g.next(1))
                    if s >= 2:
                        values(g, s - 2)
                    elif not g.first:
                        values(g.next(-1), NSLOT - 2 + s)

            for a in range(NSLOT):
                for h in range(GH):
                    max_tile(Group(0, 0), a, h)
            for a in range(AHEAD):
                for h in range(GH):
                    max_tile(Group(0, 1), a, h)
                if a == 0:
                    turn_m(Group(0, 0))
            pe.wait_ge(kz_ready, NBUF * GH)
            pe.wait_ge(qz_ready, NBUF)
            groups(pe, step)
            for s in (NSLOT - 2, NSLOT - 1):
                values(Group(0, NG - 1), s)


def stage_c(nc, psum, const, io, scratch):
    ident, mhalf, zero, hbias, wh, wl, hold = const
    with ExitStack() as ctx:
        ar = Arena(nc, ctx, hold)
        banks = {"T": psum[0:2], "F": [psum[2:4], psum[4:6]]}
        o_bank = psum[6:8]
        num = ar.sb("c_num", [P, KC, CHUNK])
        rden = ar.sb("c_rden", [P, KC, CHUNK])
        on = ar.sb("c_on", [P, KC, CHUNK])
        oh = ar.sb("c_oh", [P, KC, CHUNK], F32R)
        ol = ar.sb("c_ol", [P, KC, CHUNK], F32R)
        den = ar.sb("c_den", [P, T * H // P])
        x1 = ar.sb("c_x1", [P, TPC, E])
        x2 = ar.sb("c_x2", [P, TPC, E])
        out = ar.sb("c_out", [P, TPC, E])
        ln = Ffn(ar, "c_ln", (wh, wl), banks, zero)
        ffn = Experts(ar, "c_ffn", (wh, wl), banks, ln)
        den_loaded = ar.sem("c_den_loaded")
        r_ready = ar.sem("c_r_ready")
        r_stored = ar.sem("c_r_stored")
        o_loaded = ar.sem("c_o_loaded")
        x1_loaded = ar.sem("c_x1_loaded")
        on_ready = ar.sem("c_on_ready")
        oh_ready = ar.sem("c_oh_ready")
        ol_ready = ar.sem("c_ol_ready")
        op_ready = ar.sem("c_op_ready")
        x2_ready = ar.sem("c_x2_ready")
        stored = ar.sem("c_stored")
        c_ready = ar.sem("c_c_ready")
        LOADS = 16 * 2 * KC

        block = ctx.enter_context(nc.Block())

        @block.sync
        def _(sp):
            def load_o(c):
                b, half = c // 2, c % 2
                for ch in range(KC):
                    heads = bass.ds(b * H + ch * (H // KC), H // KC)
                    sp.dma_start(num[:, ch, :], scratch["o_rows"][heads, 0:D, bass.ds(half, 1)].rearrange(
                        "h d f n -> h d (f n)")).then_inc(o_loaded, 16)
                    sp.dma_start(rden[:, ch, :], scratch["r"][heads, bass.ds(half * CHUNK, CHUNK)].unsqueeze(1).to_broadcast(
                        [H // KC, D, CHUNK])).then_inc(o_loaded, 16)

            def load_x1(c):
                sp.dma_start(x1[:], scratch["x1"][bass.ds(c, 1)].rearrange("a p t e -> p (a t) e")).then_inc(x1_loaded, 16)

            def store(c):
                sp.wait_ge(ffn.out_ready, c * TPC + TPC)
                sp.dma_start(io["out"][bass.ds(c, 1)].rearrange("a p t e -> p (a t) e"), out[:]).then_inc(stored, 16)

            def step(c, prev2, nxt, nxt2):
                if nxt2:
                    sp.wait_ge(on_ready, c * KC + 2 * KC)
                    load_o(c + 2)
                if nxt:
                    sp.wait_ge(x2_ready, c * TPC + TPC)
                    load_x1(c + 1)
                if prev2:
                    store(c - 2)

            load_o(0)
            load_x1(0)
            sp.dma_start(den[:], scratch["o_rows"][EARLY:B * H, D].rearrange("h f (q n) -> h (f q) n", n=T * H // P)).then_inc(den_loaded, 16)
            sp.wait_ge(on_ready, KC)
            load_o(1)
            step(0, False, True, True)
            sp.wait_ge(r_ready, 1)
            sp.dma_start(scratch["r"][EARLY:B * H, :].rearrange("h (q n) -> (h q) n", n=T * H // P), den[:]).then_inc(r_stored, 16)
            sp.wait_ge(r_stored, 16)
            step(1, False, True, True)
            with sp.Fori(2, NCHUNK - 2) as c:
                step(c, True, True, True)
            step(NCHUNK - 2, True, True, False)
            step(NCHUNK - 1, True, False, False)
            store(NCHUNK - 2)
            store(NCHUNK - 1)
            sp.wait_ge(stored, NCHUNK * 16)

        @block.gpsimd
        def _(pool):
            pool.memset(ffn.ex[:], 0.0).then_inc(c_ready, 1)

            def divide(c, first=False):
                pool.wait_ge(o_loaded, c * LOADS + LOADS)
                if not first:
                    pool.wait_ge(ol_ready, c * KC)
                for ch in range(KC):
                    pool.tensor_tensor(on[:, ch, :], num[:, ch, :], rden[:, ch, :], ALU.mult).then_inc(on_ready, 1)

            def step(c, nxt, first=False):
                if nxt:
                    divide(c + 1)
                ln.pool_rstd(pool, c, mhalf, first)
                ffn.pool_xb(pool, c, x2, hbias, first)

            divide(0, True)
            step(0, True, True)
            with pool.Fori(1, NCHUNK - 1) as c:
                step(c, True)
            step(NCHUNK - 1, False)

        @block.scalar
        def _(act):
            act.wait_ge(c_ready, 1)

            def high(c, first=False):
                if not first:
                    act.wait_ge(op_ready, c * TPC)
                for ch in range(KC):
                    act.wait_ge(on_ready, c * KC + ch + 1)
                    act.copy(oh[:, ch, :], on[:, ch, :]).then_inc(oh_ready, 1)

            def step(c, prev, here, nxt, prev_first=False):
                k = FIRST if prev_first else c - 1

                def normalise(*tiles):
                    if here:
                        ln.act_normalise(act, c, x2, not prev, tiles)

                if prev:
                    ln.act_high(act, k)
                if nxt:
                    high(c + 1)
                if prev:
                    ffn.act_tile(act, k, 0, prev_first)
                    ffn.act_tile(act, k, 1, prev_first)
                normalise(0)
                if prev:
                    ffn.act_tile(act, k, 2, prev_first)
                normalise(1, 2)
                if prev:
                    ffn.act_tile(act, k, 3, prev_first)
                normalise(3)
                if prev:
                    ffn.act_exp(act, k)

            high(0, True)
            step(0, False, True, True)
            step(1, True, True, True, True)
            with act.Fori(2, NCHUNK - 1) as c:
                step(c, True, True, True)
            step(NCHUNK - 1, True, True, False)
            step(NCHUNK, True, False, False)

        @block.vector
        def _(dve):
            def low(c, ch):
                dve.wait_ge(oh_ready, c * KC + ch + 1)
                dve.tensor_tensor(ol[:, ch, :], on[:, ch, :], oh[:, ch, :].bitcast(F32),
                                  ALU.subtract).then_inc(ol_ready, 1)

            def output(c, t):
                if t == 0:
                    if not (isinstance(c, int) and c == 0):
                        dve.wait_ge(stored, c * 16)
                ffn.dve_out(dve, c, t, out)

            def step(c, prev2, prev, here, nxt):
                if here:
                    dve.wait_ge(x1_loaded, c * 16 + 16)
                    if prev:
                        dve.wait_ge(ln.xn_ready, c * TPC)
                        dve.wait_ge(ffn.xb_ready, c * TPC)
                for t in range(TPC):
                    if here:
                        dve.wait_ge(op_ready, c * TPC + t + 1)
                        dve.tensor_tensor(x2[:, t, :], o_bank[t % 2][:, (t // 2) * E:(t // 2 + 1) * E], x1[:, t, :],
                                          ALU.add).then_inc(x2_ready, 1)
                    if prev2 and t == 0:
                        ffn.dve_gate(dve, c - 2)
                    if here:
                        dve.wait_ge(x2_ready, c * TPC + t + 1)
                        ln.dve_stats(dve, c, t, x2)
                    if prev and t == 1:
                        ln.dve_low(dve, c - 1)
                if here:
                    ln.dve_aggregate(dve, c, not prev)
                if prev2:
                    output(c - 2, 0)
                for t in range(TPC):
                    if prev2 and t + 1 < TPC:
                        output(c - 2, t + 1)
                    if prev:
                        if prev2:
                            dve.wait_ge(ffn.out_ready, c * TPC - 2 * TPC + t + 1)
                        ffn.dve_tile(dve, c - 1, t)
                    if nxt and t < KC:
                        low(c + 1, t)
                if prev:
                    ffn.dve_logits(dve, c - 1)

            for ch in range(KC):
                low(0, ch)
            step(0, False, False, True, True)
            dve.wait_ge(den_loaded, 16)
            dve.reciprocal(den[:], den[:]).then_inc(r_ready, 1)
            step(1, False, True, True, True)
            step(2, True, True, True, True)
            with dve.Fori(3, NCHUNK - 1) as c:
                step(c, True, True, True, True)
            step(NCHUNK - 1, True, True, True, False)
            step(NCHUNK, True, True, False, False)
            step(NCHUNK + 1, True, False, False, False)

        @block.tensor
        def _(pe):
            def project_out(c, later, tiles):
                if tiles[0] == 0:
                    pe.wait_ge(ol_ready, c * KC + KC)
                    if later:
                        pe.wait_ge(x2_ready, c * TPC)
                cols = slice(W_OUT, W_OUT + E)
                for t in tiles:
                    if t >= 2:
                        pe.wait_ge(x2_ready, c * TPC + t - 1)
                    toks = slice(t * P, (t + 1) * P)
                    project(pe, o_bank[t % 2][:, (t // 2) * E:(t // 2 + 1) * E],
                            [oh[:, ch, toks] for ch in range(KC)], [ol[:, ch, toks] for ch in range(KC)],
                            [wh[:, ch, cols] for ch in range(KC)],
                            [wl[:, ch, cols] for ch in range(KC)]).then_inc(op_ready, 1)

            def step(c, prev, here=True, prev_first=False):
                k = FIRST if prev_first else c - 1
                if here:
                    project_out(c, prev, [0])
                if prev:
                    ln.pe_transpose(pe, k, ident)
                if here:
                    project_out(c, prev, range(1, TPC))
                if prev:
                    for t in range(TPC):
                        ffn.pe_tile(pe, k, t)

            step(0, False)
            step(1, True, prev_first=True)
            with pe.Fori(2, NCHUNK) as c:
                step(c, True)
            step(NCHUNK, True, here=False)


def macaron(nc, x, wqkv_t, wsh_t, wex_t, wgate, wout_t, bias, out):
    scr_qk = nc.dram_tensor("scr_qk", [B, 2, 2, E, T // CHUNK, CHUNK], F32).ap()
    scr_v = nc.dram_tensor("scr_v", [NCHUNK, TPC, P, E], F32).ap()
    scr_x1 = nc.dram_tensor("scr_x1", [NCHUNK, P, TPC, E], F32).ap()
    scr_o = nc.dram_tensor("scr_o", [NG, P, 2, CHUNK], F32).ap()
    scr_r = nc.dram_tensor("scr_r", [B * H, T], F32).ap()
    scratch = {
        "qk": scr_qk,
        "qk_b": scr_qk.rearrange("b k q (g h d) f n -> b k q g h d (f n)", g=GPB, h=GH),
        "v": scr_v,
        "v_b": scr_v.rearrange("(b f) t p (g n) -> b (f t) p g n", f=2, g=GPB),
        "x1": scr_x1,
        "o": scr_o,
        "o_rows": scr_o.rearrange("g (h r) f n -> (g h) r f n", h=GH),
        "r": scr_r,
    }
    io = {
        "x": x.rearrange("(c t p) e -> c p t e", t=TPC, p=P),
        "out": out.rearrange("(c t p) e -> c p t e", t=TPC, p=P),
        "weights": [(wqkv_t, W_QK), (wsh_t, W_SH), (wex_t, W_EX), (wgate, W_EX + E), (wout_t, W_OUT)],
        "bias": bias,
    }
    with ExitStack() as ctx:
        ar = Arena(nc, ctx)
        psum = [ctx.enter_context(nc.psum_tensor(f"bank{n}", [P, BANK], F32)) for n in range(8)]
        ident = ar.sb("ident", [P, P])
        mhalf = ar.sb("mhalf", [P, TPC])
        zero = ar.sb("zero", [P, TPC])
        hbias = ar.sb("hbias", [P, E])
        wh = ar.sb("wh", [P, KC, WCOLS], F32R)
        wl = ar.sb("wl", [P, KC, WCOLS], F32R)
        const = (ident, mhalf, zero, hbias, wh, wl, Hold(ar))
        stage_a(nc, psum, const, io, scratch)
        stage_b(nc, psum, const, scratch)
        stage_c(nc, psum, const, io, scratch)


def kernel(**inputs):
    import numpy as np
    import concourse.bacc as bacc
    from concourse.bass_utils import run_bass_kernel_spmd

    x = np.asarray(inputs["L0_attn_query"])
    arrays = {
        "x": np.ascontiguousarray(x.reshape(B * T, E)),
        "wqkv_t": np.ascontiguousarray(np.asarray(inputs["L0_attn_in_proj_weight"]).T),
        "wsh_t": np.ascontiguousarray(np.asarray(inputs["L0_ffn_W_shared"]).T),
        "wex_t": np.ascontiguousarray(np.asarray(inputs["L0_ffn_W_expert"]).T),
        "wgate": np.ascontiguousarray(np.asarray(inputs["L0_ffn_W_gate"])),
        "wout_t": np.ascontiguousarray(np.asarray(inputs["L0_attn_out_proj_weight"]).T),
        "bias": np.ascontiguousarray(np.asarray(inputs["L0_ffn_bias"])),
    }
    nc = bacc.Bacc("TRN2", target_bir_lowering=False, num_devices=1)
    nc.disable_value_cache = True
    args = [nc.dram_tensor(n, a.shape, mybir.dt.from_np(a.dtype), kind="ExternalInput").ap() for n, a in arrays.items()]
    out = nc.dram_tensor("out", [B * T, E], F32, kind="ExternalOutput").ap()
    macaron(nc, *args, out)
    got = run_bass_kernel_spmd(nc, [arrays], core_ids=[0])
    return got.results[0]["out"].reshape(B, T, E)
```

```python
from contextlib import ExitStack

import concourse.bass as bass
from concourse import mybir

F32 = mybir.dt.float32
F32R = mybir.dt.float32r
BF16 = mybir.dt.bfloat16
ALU = mybir.AluOpType
ACT = mybir.ActivationFunctionType
AX = mybir.AxisListType

P = 128
B, T, E = 8, 1024, 256
H, D = 16, 16
NEXP = 7
EPS = 1e-5
CHUNK = 512
TPC = CHUNK // P
NCHUNK = B * T // CHUNK
KC = E // P
GH = 4
NG = B * H // GH
GPB = H // GH
KT = T // P
BANK = 512
YL = E + NEXP + 1

W_QK, W_V, W_SH, W_EX, W_OUT = 0, 2 * E, 3 * E, 4 * E, 4 * E + YL
WCOLS = W_OUT + E

W_FFN, W_QKV, W_PROJ = slice(W_SH, W_OUT), slice(W_QK, W_SH), slice(W_OUT, WCOLS)

SROWS = 4 * D
SROWS_M = SROWS + 2
NBUF = 3
AHEAD = 3
MASKED = -1.0e38

SLOTS = [
    [(0, 0, 512, 0)],
    [(0, 512, 512, 0)],
    [(1, 128, 384, 0), (7, 896, 128, 384)],
    [(2, 256, 256, 0), (6, 768, 256, 256)],
    [(3, 384, 128, 0), (5, 640, 384, 128)],
    [(1, 512, 512, 0)],
    [(2, 512, 512, 0)],
    [(3, 512, 512, 0)],
    [(4, 512, 512, 0)],
]
NSLOT = len(SLOTS)
TILES = NSLOT * GH
DIAG = [[off for j, q0, n, off in s if q0 == j * P] for s in SLOTS]
DIAG_SLOTS = [s for s in range(NSLOT) if DIAG[s]]
LOW_DONE, HIGH_DONE = 4, 8

MAX_SLOTS = [
    [(3, 0, 512, 0)],
    [(7, 512, 512, 0)],
    [(7, 0, 512, 0)],
    [(6, 0, 512, 0)],
    [(5, 0, 512, 0)],
    [(4, 0, 512, 0)],
    [(2, 0, 384, 0), (0, 0, 128, 384)],
    [(6, 512, 384, 0), (4, 512, 128, 384)],
    [(1, 0, 256, 0), (5, 512, 256, 256)],
]
EARLY = (B - 1) * H
SB = 3
M_BANK = 2
TURN_NEXT = SB * (GH // SB) + M_BANK


class Arena:

    def __init__(self, nc, ctx, hold=None):
        self.nc, self.ctx, self.hold = nc, ctx, hold

    def sb(self, name, shape, dt=F32):
        return self.ctx.enter_context(self.nc.sbuf_tensor(name, shape, dt))

    def sem(self, name):
        return self.ctx.enter_context(self.nc.semaphore(name))


class Chain:

    def __init__(self, eng, sem, base):
        self.eng, self.sem, self.base, self.n = eng, sem, base, 0

    def __call__(self, ins):
        ins.then_inc(self.sem, 1)
        self.n += 1
        self.eng.wait_ge(self.sem, self.base + self.n)


class Hold:

    COLS = 8

    def __init__(self, ar):
        self.dve_out = ar.sb("hold_dve", [P, self.COLS])
        self.pool_out = ar.sb("hold_pool", [P, self.COLS])

    def dve(self, dve, col):
        dve.memset(self.dve_out[:, col:col + 1], 0.0)

    def pool(self, pool, col, zero):
        pool.tensor_tensor(self.pool_out[:, col:col + 1], zero[:, 0:1], zero[:, 1:2], ALU.add)


def project(pe, out, lh, ll, rh, rl):
    terms = [(a[ch], b[ch]) for ch in range(KC) for a, b in ((lh, rh), (lh, rl), (ll, rh))]
    for n, (a, b) in enumerate(terms):
        last = pe.matmul(out, a, b, start=(n == 0), stop=(n == len(terms) - 1))
    return last


def loop(eng, lo, hi):
    return eng.bass.Fori(lo, hi, engines=(eng.engine,), hint_back_edge=True)


def pairs(eng, lo, hi, step):
    if (hi - lo) % 2:
        step(lo)
        lo += 1
    with loop(eng, 0, (hi - lo) // 2) as r:
        for k in range(2):
            step(r * 2 + (lo + k))


GATE_LINKS = 2 + TPC + 4


class Norm:

    def __init__(self, ar, name, banks, zero, col=0):
        self.banks, self.hold = banks, ar.hold
        sb, sem = (lambda n, s, d=F32: ar.sb(f"{name}_{n}", s, d)), (lambda n: ar.sem(f"{name}_{n}"))
        self.stats = sb("stats", [P, TPC, 6])
        self.mv = sb("mv", [P, TPC, 2])
        self.veps = sb("veps", [P, TPC])
        self.nmean = sb("nmean", [P, TPC])
        self.zero, self.col = zero, col
        self.rstd = sb("rstd", [P, TPC])
        self.nbias = sb("nbias", [P, TPC])
        self.xn = sb("xn", [P, TPC, E])
        self.xh = sb("xh", [P, KC, CHUNK], F32R)
        self.xl = sb("xl", [P, KC, CHUNK], F32R)
        self.bn_done = sem("bn_done")
        self.mv_ready = sem("mv_ready")
        self.pool_chain = sem("pool_chain")
        self.xn_ready = sem("xn_ready")
        self.t_ready = sem("t_ready")
        self.xh_ready = sem("xh_ready")
        self.xl_ready = sem("xl_ready")

    def dve_stats(self, dve, k, t, x):
        dve.bn_stats(self.stats[:, t, :], x[:, t, :]).then_inc(self.bn_done, 1)

    def dve_aggregate(self, dve, k, first=False):
        dve.wait_ge(self.bn_done, k * TPC + TPC)
        if not first:
            dve.wait_ge(self.xn_ready, k * TPC)
        self.hold.dve(dve, self.col)
        for t in range(TPC):
            dve.bn_aggr(self.mv[:, t, :], self.stats[:, t, :]).then_inc(self.mv_ready, 1)

    def pool_rstd(self, pool, k, mhalf, first=False):
        pool.wait_ge(self.mv_ready, k * TPC + TPC)
        if not first:
            pool.wait_ge(self.xn_ready, k * TPC)
        pool.tensor_tensor(self.nmean[:], self.zero[:], self.mv[:, :, 0], ALU.subtract).then_inc(self.pool_chain, 1)
        pool.tensor_scalar(self.veps[:], self.mv[:, :, 1], EPS, None, ALU.add).then_inc(self.pool_chain, 1)
        pool.wait_ge(self.pool_chain, k * 4 + 2)
        pool.tensor_tensor(self.rstd[:], self.veps[:], mhalf[:], ALU.pow).then_inc(self.pool_chain, 1)
        pool.wait_ge(self.pool_chain, k * 4 + 3)
        pool.tensor_tensor(self.nbias[:], self.nmean[:], self.rstd[:], ALU.mult).then_inc(self.pool_chain, 1)

    def act_normalise(self, act, k, x, first=False, tiles=range(TPC)):
        if tiles[0] == 0:
            act.wait_ge(self.pool_chain, k * 4 + 4)
            if not first:
                act.wait_ge(self.t_ready, k * KC)
        for t in tiles:
            act.activation(self.xn[:, t, :], x[:, t, :], ACT.Identity, scale=self.rstd[:, t:t + 1],
                           bias=self.nbias[:, t:t + 1]).then_inc(self.xn_ready, 1)

    def pe_transpose(self, pe, k, ident):
        for ch in range(KC):
            for t in range(TPC):
                if ch == 0:
                    pe.wait_ge(self.xn_ready, k * TPC + t + 1)
                last = pe.transpose(self.banks["T"][ch][:, t * P:(t + 1) * P],
                                    self.xn[:, t, ch * P:(ch + 1) * P], ident[:])
            last.then_inc(self.t_ready, 1)

    def act_high(self, act, k):
        for ch in range(KC):
            act.wait_ge(self.t_ready, k * KC + ch + 1)
            act.copy(self.xh[:, ch, :], self.banks["T"][ch][:]).then_inc(self.xh_ready, 1)

    def dve_low(self, dve, k, chs=range(KC)):
        for ch in chs:
            dve.wait_ge(self.xh_ready, k * KC + ch + 1)
            dve.tensor_tensor(self.xl[:, ch, :], self.banks["T"][ch][:], self.xh[:, ch, :].bitcast(F32),
                              ALU.subtract).then_inc(self.xl_ready, 1)

    def tile(self, t):
        cols = slice(t * P, (t + 1) * P)
        return [self.xh[:, ch, cols] for ch in range(KC)], [self.xl[:, ch, cols] for ch in range(KC)]

    def whole(self):
        return [self.xh[:, ch, :] for ch in range(KC)], [self.xl[:, ch, :] for ch in range(KC)]


class Experts:

    def __init__(self, ar, name, w, banks, ln):
        self.w, self.banks, self.ln = w, banks, ln
        sb, sem = (lambda n, s, d=F32: ar.sb(f"{name}_{n}", s, d)), (lambda n: ar.sem(f"{name}_{n}"))
        self.xb = sb("xb", [P, TPC, E])
        self.acc = sb("acc", [P, TPC, E])
        self.yl = sb("yl", [P, TPC, YL])
        self.lmax = sb("lmax", [P, TPC])
        self.dl = sb("dl", [P, TPC, NEXP])
        self.ex = sb("ex", [P, TPC, 8])
        self.top = sb("top", [P, TPC, 8])
        self.den = sb("den", [P, TPC])
        self.rden = sb("rden", [P, TPC])
        self.w2 = sb("w2", [P, TPC, 2])
        self.wsum = sb("wsum", [P, TPC])
        self.ffn_ready = sem("ffn_ready")
        self.yl_ready = sem("yl_ready")
        self.acc_ready = sem("acc_ready")
        self.xb_ready = sem("xb_ready")
        self.gate_chain = sem("gate_chain")
        self.ex_ready = sem("ex_ready")
        self.out_ready = sem("out_ready")

    def pe_tile(self, pe, k, t):
        n = k * TPC + t
        sh, ex = self.banks["F"][t % 2]
        if t == 0:
            pe.wait_ge(self.ln.xl_ready, k * KC + KC)
        if not (k is FIRST and t < 2):
            pe.wait_ge(self.yl_ready, n - 1)
            pe.wait_ge(self.acc_ready, n - 1)
        lh, ll = self.ln.tile(t)
        wh, wl = self.w
        cols = slice(W_EX, W_EX + YL)
        project(pe, ex[:, 0:YL], lh, ll, [wh[:, ch, cols] for ch in range(KC)], [wl[:, ch, cols] for ch in range(KC)])
        cols = slice(W_SH, W_SH + E)
        project(pe, sh[:, 0:E], lh, ll, [wh[:, ch, cols] for ch in range(KC)],
                [wl[:, ch, cols] for ch in range(KC)]).then_inc(self.ffn_ready, 1)

    def act_tile(self, act, k, t, first=False):
        act.wait_ge(self.ffn_ready, k * TPC + t + 1)
        if not first:
            act.wait_ge(self.out_ready, k * TPC - TPC + t + 1)
        act.mul(self.yl[:, t, :], self.banks["F"][t % 2][1][:, 0:YL], 0.5).then_inc(self.yl_ready, 1)

    def dve_tile(self, dve, k, t):
        dve.wait_ge(self.ffn_ready, k * TPC + t + 1)
        dve.wait_ge(self.xb_ready, k * TPC + t + 1)
        dve.scalar_tensor_tensor(out=self.acc[:, t, :], in0=self.banks["F"][t % 2][0][:, 0:E], scalar=0.5,
                                 in1=self.xb[:, t, :], op0=ALU.mult, op1=ALU.add).then_inc(self.acc_ready, 1)

    def dve_logits(self, dve, k):
        ch = Chain(dve, self.gate_chain, k * GATE_LINKS)
        dve.wait_ge(self.yl_ready, k * TPC + TPC)
        logits = self.yl[:, :, E:E + NEXP]
        ch(dve.tensor_reduce(self.lmax[:], logits, AX.X, ALU.max))
        ch(dve.tensor_tensor(self.dl[:], logits, self.lmax[:].unsqueeze(2).to_broadcast([P, TPC, NEXP]), ALU.subtract))

    def dve_gate(self, dve, k):
        ch = Chain(dve, self.gate_chain, k * GATE_LINKS)
        ch.n = 2
        dve.wait_ge(self.ex_ready, k + 1)
        self.ln.hold.dve(dve, 2)
        for t in range(TPC):
            last = dve.max(self.top[:, t, :], self.ex[:, t, :])
            if t < TPC - 1:
                last.then_inc(self.gate_chain, 1)
                ch.n += 1
        ch(last)
        ch(dve.tensor_tensor(self.den[:], self.top[:, :, 0], self.top[:, :, 1], ALU.add))
        ch(dve.reciprocal(self.rden[:], self.den[:]))
        ch(dve.tensor_tensor(self.w2[:], self.top[:, :, 0:2], self.rden[:].unsqueeze(2).to_broadcast([P, TPC, 2]), ALU.mult))
        ch(dve.tensor_tensor(self.wsum[:], self.w2[:, :, 0], self.w2[:, :, 1], ALU.add))
        assert ch.n == GATE_LINKS

    def act_exp(self, act, k):
        act.wait_ge(self.gate_chain, k * GATE_LINKS + 2)
        act.activation(self.ex[:, :, 0:NEXP], self.dl[:], ACT.Exp, scale=2.0).then_inc(self.ex_ready, 1)

    def dve_out(self, dve, k, t, out):
        if t == 0:
            dve.wait_ge(self.acc_ready, k * TPC + TPC)
        dve.scalar_tensor_tensor(out=out[:, t, :], in0=self.yl[:, t, 0:E], scalar=self.wsum[:, t:t + 1],
                                 in1=self.acc[:, t, :], op0=ALU.mult, op1=ALU.add).then_inc(self.out_ready, 1)

    def pool_xb(self, pool, k, x, hbias, first=False):
        for t in range(TPC):
            if not first:
                pool.wait_ge(self.acc_ready, k * TPC - TPC + t + 1)
            pool.tensor_tensor(self.xb[:, t, :], x[:, t, :], hbias[:], ALU.add).then_inc(self.xb_ready, 1)


class _First(int):
    pass


FIRST = _First(0)


class Ahead:

    GROUPS = 2
    STACK = 16 * 8

    def __init__(self, ar):
        self.qs = [ar.sb(f"qs{n}", [P, GH, T], F32R) for n in range(self.GROUPS)]
        self.ks = [ar.sb(f"ks{n}", [P, GH, T], F32R) for n in range(self.GROUPS)]
        self.mask = ar.sb("mask", [P, BANK])
        self.stacked = [ar.sem(f"stacked{n}") for n in range(NBUF)]
        self.ready = ar.sem("rows_ready")

    def load(self, sp, scratch, i, qs, ks, sem):
        b, gg = i // GPB, i % GPB
        for kind, dst, order in ((0, qs, (0, 0, 1, 1)), (1, ks, (0, 1, 0, 1))):
            for n, part in enumerate(order):
                src = scratch["qk_b"][bass.ds(b, 1), kind, part, bass.ds(gg, 1)]
                sp.dma_start(dst[n * D:(n + 1) * D, :, :].bitcast(F32),
                             src.rearrange("a g h d n -> d (a g h) n")).then_inc(sem, 16)

    @staticmethod
    def rows(chain, pool, qs, ks):
        chain(pool.memset(qs[SROWS:P, :, :].bitcast(F32), 0.0))
        chain(pool.memset(ks[SROWS:P, :, :].bitcast(F32), 0.0))
        chain(pool.memset(ks[SROWS:SROWS_M, :, :].bitcast(F32), 1.0))

    def pool_mask(self, pool):
        chain = Chain(pool, self.ready, 0)
        chain(pool.memset(self.mask[:], 0.0))
        diag = self.mask[:, BANK - P:BANK]
        chain(pool.affine_select(out=diag, in_=diag, compare_op=ALU.is_ge, fill=MASKED, base=0,
                                 pattern=[[-1, P]], channel_multiplier=1))

    def pool_rows(self, pool, n):
        self.rows(Chain(pool, self.ready, 2 + 3 * n), pool, self.qs[n], self.ks[n])


class Attended:

    LOADS = 16 * 2 * KC

    def __init__(self, ar):
        self.num = ar.sb("num", [P, KC, CHUNK])
        self.rden = ar.sb("rden", [P, KC, CHUNK])
        self.on = ar.sb("on", [P, KC, CHUNK])
        self.x1 = ar.sb("x1", [P, TPC, E])
        self.o_loaded = ar.sem("o_loaded")
        self.x1_loaded = ar.sem("x1_loaded")
        self.on_ready = ar.sem("on_ready")

    def load_num(self, sp, scratch, c):
        for ch in range(KC):
            heads = bass.ds(c // 2 * H + ch * (H // KC), H // KC)
            sp.dma_start(self.num[:, ch, :], scratch["o_rows"][heads, 0:D, bass.ds(c % 2, 1)].rearrange(
                "h d f n -> h d (f n)")).then_inc(self.o_loaded, 16)

    def load_rden(self, sp, scratch, c):
        for ch in range(KC):
            heads = bass.ds(c // 2 * H + ch * (H // KC), H // KC)
            sp.dma_start(self.rden[:, ch, :], scratch["r"][heads, bass.ds(c % 2 * CHUNK, CHUNK)].unsqueeze(1).to_broadcast(
                [H // KC, D, CHUNK])).then_inc(self.o_loaded, 16)

    def load_x1(self, sp, scratch, c):
        sp.dma_start(self.x1[:], scratch["x1"][bass.ds(c, 1)].rearrange("a p t e -> p (a t) e")).then_inc(self.x1_loaded, 16)


def stage_a(nc, psum, const, io, scratch, ahead):
    ident, mhalf, zero, hbias, wh, wl, hold = const
    with ExitStack() as ctx:
        ar = Arena(nc, ctx, hold)
        banks = {"T": psum[0:2], "F": [psum[2:4], psum[4:6]], "Q": psum[6:8]}
        x = ar.sb("a_x", [P, TPC, E])
        x1 = ar.sb("a_x1", [P, TPC, E])
        qk = ar.sb("a_qk", [P, 2 * KC, 2, CHUNK], F32R)
        v = ar.sb("a_v", [P, TPC, E])
        stage = ar.sb("a_stage", [P, KC, WCOLS])
        brow = ar.sb("a_brow", [P, E])
        ln1 = Norm(ar, "a_ln1", banks, zero)
        ln2 = Norm(ar, "a_ln2", banks, zero, 1)
        ffn = Experts(ar, "a_ffn", (wh, wl), banks, ln1)
        wf_loaded = ar.sem("wf_loaded")
        wp_loaded = ar.sem("wp_loaded")
        brow_loaded = ar.sem("brow_loaded")
        pad_ready = ar.sem("pad_ready")
        wh_ready = ar.sem("wh_ready")
        wl_ready = ar.sem("wl_ready")
        b_ready = ar.sem("b_ready")
        c_ready = ar.sem("c_ready")
        x_loaded = ar.sem("x_loaded")
        x1_stored = ar.sem("x1_stored")
        qk_stored = ar.sem("qk_stored")
        v_stored = ar.sem("v_stored")
        qkv_ready = ar.sem("qkv_ready")
        qh_ready = ar.sem("qh_ready")
        ql_ready = ar.sem("ql_ready")
        NQK, QKV = 2 * KC, 2 * KC + TPC // 2
        PROJ = [("qk", 0), ("qk", 1), ("v", 0), ("v", 1), ("qk", 2), ("qk", 3)]
        PROJ_EARLY = 3
        proj_bank = [*banks["F"][0], *banks["F"][1], *banks["Q"]]

        block = ctx.enter_context(nc.Block())

        @block.sync
        def _(sp):
            def load_weights(names, sem):
                for name in names:
                    src, col = io["weights"][name]
                    n = src.shape[1]
                    sp.dma_start(stage[:, :, col:col + n], src.rearrange("(k p) n -> p k n", p=P)).then_inc(sem, 16)

            def load(c):
                sp.dma_start(x[:], io["x"][bass.ds(c, 1)].rearrange("a p t e -> p (a t) e")).then_inc(x_loaded, 16)

            def store_x1(c):
                sp.wait_ge(ffn.out_ready, c * TPC + TPC)
                sp.dma_start(scratch["x1"][bass.ds(c, 1)].rearrange("a p t e -> p (a t) e"), x1[:]).then_inc(x1_stored, 16)

            def store_qkv(c):
                for j in range(NQK):
                    sp.wait_ge(ql_ready, c * NQK + j + 1)
                    dst = scratch["qk"][bass.ds(c // 2, 1), j // KC, :, (j % KC) * P:(j % KC + 1) * P, bass.ds(c % 2, 1)]
                    sp.dma_start(dst.rearrange("a q r f n -> r (a q) (f n)"), qk[:, j, :, :].bitcast(F32)).then_inc(qk_stored, 16)
                sp.wait_ge(qh_ready, c * QKV + QKV)
                sp.dma_start(scratch["v"][bass.ds(c, 1)].rearrange("a t p e -> p (a t) e"), v[:]).then_inc(v_stored, 16)

            def step(c, prev, nxt2):
                if nxt2:
                    sp.wait_ge(ln1.xn_ready, c * TPC + 2 * TPC)
                    sp.wait_ge(ffn.xb_ready, c * TPC + 2 * TPC)
                    load(c + 2)
                store_x1(c)
                if prev:
                    store_qkv(c - 1)

            load(0)
            load_weights(("shared", "expert", "gate"), wf_loaded)
            sp.dma_start(brow[:], io["bias"].rearrange("(a n) -> a n", a=1).to_broadcast([P, E])).then_inc(brow_loaded, 16)
            load_weights(("qkv", "out"), wp_loaded)
            sp.wait_ge(ln1.xn_ready, TPC)
            sp.wait_ge(ffn.xb_ready, TPC)
            load(1)
            step(0, False, True)
            with loop(sp, 1, NCHUNK - 1 - ahead.GROUPS) as c:
                step(c, True, True)
            sp.wait_ge(qk_stored, T // CHUNK * NQK * 16)
            for g in range(ahead.GROUPS):
                c = NCHUNK - 1 - ahead.GROUPS + g
                step(c, True, c < NCHUNK - 2)
                ahead.load(sp, scratch, g, ahead.qs[g], ahead.ks[g], ahead.stacked[g])
            step(NCHUNK - 1, True, False)
            store_qkv(NCHUNK - 1)
            sp.wait_ge(x1_stored, NCHUNK * 16)
            sp.wait_ge(qk_stored, NCHUNK * NQK * 16)
            sp.wait_ge(v_stored, NCHUNK * 16)

        @block.gpsimd
        def _(pool):
            pool.memset(ident[:], 0.0).then_inc(c_ready, 1)
            pool.memset(mhalf[:], -0.5).then_inc(c_ready, 1)
            pool.memset(zero[:], 0.0).then_inc(c_ready, 1)
            pool.memset(ffn.ex[:], 0.0).then_inc(c_ready, 1)
            pool.memset(stage[:, :, W_EX + E + NEXP:W_EX + YL], 0.0).then_inc(pad_ready, 1)
            pool.wait_ge(c_ready, 4)
            pool.affine_select(out=ident[:], in_=ident[:], compare_op=ALU.not_equal, fill=1.0, base=0,
                               pattern=[[-1, P]], channel_multiplier=1).then_inc(c_ready, 1)
            pool.wait_ge(x_loaded, 16)
            pool.wait_ge(b_ready, 1)
            ln1.pool_rstd(pool, 0, mhalf, first=True)
            ffn.pool_xb(pool, 0, x, hbias, first=True)

            def step(c, nxt):
                if nxt:
                    ln1.pool_rstd(pool, c + 1, mhalf)
                    ffn.pool_xb(pool, c + 1, x, hbias)
                ln2.pool_rstd(pool, c, mhalf, first=(c is FIRST))

            step(FIRST, True)
            pool.wait_ge(ln2.pool_chain, 4)
            ahead.pool_mask(pool)
            step(1, True)
            pool.wait_ge(ln2.pool_chain, 8)
            ahead.pool_rows(pool, 0)
            with loop(pool, 2, NCHUNK - 1) as c:
                step(c, True)
            step(NCHUNK - 1, False)
            pool.wait_ge(ln2.pool_chain, 4 * NCHUNK)
            ahead.pool_rows(pool, 1)

        @block.scalar
        def _(act):
            act.preload_act_table(ACT.Exp)

            def high_weights(cols):
                act.copy(wh[:, :, cols], stage[:, :, cols]).then_inc(wh_ready, 1)

            act.wait_ge(wf_loaded, 3 * 16)
            act.wait_ge(pad_ready, 1)
            high_weights(W_FFN)
            act.wait_ge(x_loaded, 16)
            ln1.act_normalise(act, 0, x, first=True)
            ln1.act_high(act, 0)

            def high(c, j, first):
                kind, i = PROJ[j]
                act.wait_ge(qkv_ready, c * QKV + j + 1)
                if kind == "v":
                    if not first:
                        act.wait_ge(v_stored, c * 16)
                    act.copy(v[:, 2 * i:2 * i + 2, :], proj_bank[j][:].rearrange("p (t e) -> p t e", t=2)).then_inc(qh_ready, 1)
                else:
                    if not first:
                        act.wait_ge(qk_stored, c * NQK * 16)
                    act.mul(qk[:, i, 0, :], proj_bank[j][:], 0.25 if i < KC else 1.0).then_inc(qh_ready, 1)

            def step(c, prev, nxt, prev_first=False):
                first = c is FIRST

                def norm2(*tiles):
                    if prev:
                        ln2.act_normalise(act, FIRST if prev_first else c - 1, x1, prev_first, tiles)

                def norm1(*tiles):
                    if nxt:
                        ln1.act_normalise(act, c + 1, x, False, tiles)

                norm2(0)
                ffn.act_tile(act, c, 0, first)
                norm2(1, 2)
                ffn.act_tile(act, c, 1, first)
                norm2(3)
                ffn.act_tile(act, c, 2, first)
                if prev:
                    ln2.act_high(act, c - 1)
                norm1(0)
                ffn.act_tile(act, c, 3, first)
                norm1(1)
                ffn.act_exp(act, c)
                norm1(2, 3)
                if first:
                    act.wait_ge(wp_loaded, 2 * 16)
                    high_weights(W_QKV)
                    high_weights(W_PROJ)
                if prev:
                    for j in range(PROJ_EARLY):
                        high(c - 1, j, prev_first)
                if nxt:
                    ln1.act_high(act, c + 1)
                if prev:
                    for j in range(PROJ_EARLY, QKV):
                        high(c - 1, j, prev_first)

            step(FIRST, False, True)
            step(1, True, True, True)
            with loop(act, 2, NCHUNK - 1) as c:
                step(c, True, True)
            step(NCHUNK - 1, True, False)
            ln2.act_normalise(act, NCHUNK - 1, x1)
            ln2.act_high(act, NCHUNK - 1)
            for j in range(QKV):
                high(NCHUNK - 1, j, False)

        @block.vector
        def _(dve):
            def low_weights(cols, n):
                dve.wait_ge(wh_ready, n)
                dve.tensor_tensor(wl[:, :, cols], stage[:, :, cols], wh[:, :, cols].bitcast(F32), ALU.subtract).then_inc(wl_ready, 1)

            def low(c, i):
                j = PROJ.index(("qk", i))
                dve.wait_ge(qh_ready, c * QKV + j + 1)
                dve.scalar_tensor_tensor(out=qk[:, i, 1, :], in0=proj_bank[j][:], scalar=0.25 if i < KC else 1.0,
                                         in1=qk[:, i, 0, :].bitcast(F32), op0=ALU.mult,
                                         op1=ALU.subtract).then_inc(ql_ready, 1)

            def step(c, prev, nxt):
                ffn.dve_tile(dve, c, 0)
                if nxt:
                    dve.wait_ge(x_loaded, c * 16 + 32)
                    for t in (0, 1):
                        ln1.dve_stats(dve, c + 1, t, x)
                ffn.dve_tile(dve, c, 1)
                if nxt:
                    for t in (2, 3):
                        ln1.dve_stats(dve, c + 1, t, x)
                    ln1.dve_aggregate(dve, c + 1)
                ffn.dve_tile(dve, c, 2)
                if prev:
                    ln2.dve_low(dve, c - 1)
                ffn.dve_tile(dve, c, 3)
                ffn.dve_logits(dve, c)
                ffn.dve_gate(dve, c)
                if prev:
                    low(c - 1, 0)
                    dve.wait_ge(x1_stored, c * 16)
                    dve.wait_ge(ln2.xn_ready, c * TPC)
                for t in range(TPC):
                    ffn.dve_out(dve, c, t, x1)
                    if t:
                        dve.wait_ge(ffn.out_ready, c * TPC + t)
                        ln2.dve_stats(dve, c, t - 1, x1)
                dve.wait_ge(ffn.out_ready, c * TPC + TPC)
                ln2.dve_stats(dve, c, TPC - 1, x1)
                ln2.dve_aggregate(dve, c, first=(c is FIRST))
                if prev:
                    low(c - 1, 1)
                if nxt:
                    ln1.dve_low(dve, c + 1)
                if prev:
                    low(c - 1, 2)
                    low(c - 1, 3)

            dve.wait_ge(x_loaded, 16)
            for t in range(TPC):
                ln1.dve_stats(dve, 0, t, x)
            ln1.dve_aggregate(dve, 0, first=True)
            low_weights(W_FFN, 1)
            dve.wait_ge(brow_loaded, 16)
            dve.tensor_scalar(hbias[:], brow[:], 0.5, None, ALU.mult).then_inc(b_ready, 1)
            ln1.dve_low(dve, 0)
            step(FIRST, False, True)
            low_weights(W_QKV, 2)
            low_weights(W_PROJ, 3)
            with loop(dve, 1, NCHUNK - 1) as c:
                step(c, True, True)
            step(NCHUNK - 1, True, False)
            ln2.dve_low(dve, NCHUNK - 1)
            for i in range(NQK):
                low(NCHUNK - 1, i)

        @block.tensor
        def _(pe):
            def qkv(c, js, first=False, last=False):
                th, tl = ln2.whole()
                for j in js:
                    kind, i = PROJ[j]
                    if j == 0:
                        pe.wait_ge(ln2.xl_ready, c * KC + KC)
                        if first:
                            pe.wait_ge(wl_ready, 3)
                    if last:
                        pe.wait_ge(ql_ready, c * NQK)
                        pe.wait_ge(qh_ready, c * QKV)
                    elif j in (0, 2):
                        pe.wait_ge(ffn.yl_ready, c * TPC + TPC + 3 + j // 2)
                        pe.wait_ge(ffn.acc_ready, c * TPC + TPC + 3 + j // 2)
                    elif j == 4 and not first:
                        pe.wait_ge(ql_ready, c * NQK)
                    bank = proj_bank[j]
                    if kind == "qk":
                        cols = slice(W_QK + i * P, W_QK + (i + 1) * P)
                        project(pe, bank[:], [wh[:, ch, cols] for ch in range(KC)], [wl[:, ch, cols] for ch in range(KC)],
                                th, tl).then_inc(qkv_ready, 1)
                    else:
                        cols = slice(W_V, W_V + E)
                        for t in (2 * i, 2 * i + 1):
                            lh, ll = ln2.tile(t)
                            done = project(pe, bank[:, (t % 2) * E:(t % 2 + 1) * E], lh, ll,
                                           [wh[:, ch, cols] for ch in range(KC)], [wl[:, ch, cols] for ch in range(KC)])
                        done.then_inc(qkv_ready, 1)

            def step(c, prev, nxt, prev_first=False):
                if prev and not prev_first:
                    pe.wait_ge(ql_ready, c * NQK - 2 * NQK + 2)
                ffn.pe_tile(pe, c, 0)
                if prev and not prev_first:
                    pe.wait_ge(qh_ready, c * QKV - 2 * QKV + 4)
                ffn.pe_tile(pe, c, 1)
                ffn.pe_tile(pe, c, 2)
                if prev:
                    ln2.pe_transpose(pe, c - 1, ident)
                ffn.pe_tile(pe, c, 3)
                if prev:
                    qkv(c - 1, range(PROJ_EARLY), prev_first)
                if nxt:
                    ln1.pe_transpose(pe, c + 1, ident)
                if prev:
                    qkv(c - 1, range(PROJ_EARLY, QKV), prev_first)

            pe.wait_ge(c_ready, 5)
            ln1.pe_transpose(pe, 0, ident)
            pe.wait_ge(wl_ready, 1)
            step(FIRST, False, True)
            step(1, True, True, True)
            pairs(pe, 2, NCHUNK - 1, lambda c: step(c, True, True))
            step(NCHUNK - 1, True, False)
            ln2.pe_transpose(pe, NCHUNK - 1, ident)
            qkv(NCHUNK - 1, range(QKV), last=True)


def stage_b(nc, psum, const, scratch, ahead, chunk):
    ident, _, zero, *_, hold = const
    with ExitStack() as ctx:
        ar = Arena(nc, ctx, hold)
        s_bank, m_bank, o_bank = psum[0:SB], psum[SB:2 * SB], psum[2 * SB:2 * SB + 2]
        more = range(ahead.GROUPS, NBUF)
        qs = ahead.qs + [ar.sb(f"b_qs{n}", [P, GH, T], F32R) for n in more]
        ks = ahead.ks + [ar.sb(f"b_ks{n}", [P, GH, T], F32R) for n in more]
        mask, stacked, STACK = ahead.mask, ahead.stacked, ahead.STACK
        vx = [ar.sb(f"b_vx{n}", [P, KT, GH, 2 * D]) for n in range(NBUF)]
        vin = ar.sb("b_vin", [P, KT, GH * D])
        probs = ar.sb("b_probs", [P, NBUF, GH, BANK])
        o = ar.sb("b_o", [P, 2, BANK])
        junk = ar.sb("b_junk", [P, SB, BANK], BF16)
        pm = ar.sb("b_pm", [P, NBUF, 2, GH, KT])
        mparts = ar.sb("b_mparts", [P, P // (GH * KT), GH * KT], F32R)
        mt = ar.sb("b_mt", [2 * GH * KT, P], F32R)
        den = ar.sb("b_den", [EARLY, T])

        z_ready = ar.sem("b_z_ready")
        ones_ready = ar.sem("b_ones_ready")
        rows_ready = ar.sem("b_rows_ready")
        v_loaded = ar.sem("b_v_loaded")
        vx_ready = ar.sem("b_vx_ready")
        m_tile = ar.sem("b_m_tile")
        m_read = ar.sem("b_m_read")
        m_chain = ar.sem("b_m_chain")
        m_turned = ar.sem("b_m_turned")
        m_out = ar.sem("b_m_out")
        m_placed = [ar.sem(f"b_m_placed{n}") for n in range(NBUF)]
        s_tile = ar.sem("b_s_tile")
        p_ready = ar.sem("b_p_ready")
        p_masked = ar.sem("b_p_masked")
        pv_done = ar.sem("b_pv_done")
        o_out = ar.sem("b_o_out")
        o_stored = [ar.sem(f"b_o_stored{n}") for n in range(2)]
        den_loaded = ar.sem("b_den_loaded")
        r_ready = ar.sem("b_r_ready")
        r_stored = ar.sem("b_r_stored")
        ND = len(DIAG_SLOTS)

        class Group:

            def __init__(self, r, k):
                if isinstance(r, int):
                    r, k = 0, NBUF * r + k
                self.r, self.k, self.buf = r, k, k % NBUF

            def at(self, per, more=0):
                return self.r * (NBUF * per) + (self.k * per + more)

            def turn(self, per, more=0):
                return self.r * per + (self.k // NBUF * per + more)

            def next(self, n):
                return Group(self.r, self.k + n) if not isinstance(self.r, int) else Group(0, self.k + n)

            @property
            def first(self):
                return isinstance(self.r, int) and self.k == 0

        def score_bank(t, last):
            return (s_bank + m_bank)[t % (2 * SB)] if last else s_bank[t % SB]

        def groups(eng, step):
            step(Group(0, 0), False)
            with loop(eng, 0, (NG - 2) // NBUF) as r:
                for k in range(1, NBUF + 1):
                    step(Group(r, k), False)
            step(Group(0, NG - 1), True)

        assert (NG - 2) % NBUF == 0
        block = ctx.enter_context(nc.Block())

        @block.sync
        def _(sp):
            def load(g):
                ahead.load(sp, scratch, g.at(1) % NG, qs[g.buf], ks[g.buf], stacked[g.buf])

            def load_v(g):
                i = g.at(1)
                b, gg = i // GPB, i % GPB
                sp.dma_start(vin[:], scratch["v_b"][bass.ds(b, 1), :, :, bass.ds(gg, 1)].rearrange(
                    "a k p g n -> p (a k) (g n)")).then_inc(v_loaded, 16)

            def place_m(g):
                sp.wait_ge(m_out, g.at(1, 1))
                sp.dma_start(qs[g.buf][SROWS:SROWS_M, :, :].rearrange("r h (i p) -> r (h i) p", p=P).bitcast(F32),
                             mt[:].bitcast(F32)).then_inc(m_placed[g.buf], 16)

            def store(g, half):
                sp.wait_ge(o_out, g.at(2, half + 1))
                sp.dma_start(scratch["o"][bass.ds(g.at(1), 1), :, half].rearrange("a r n -> (a r) n"),
                             o[:, half, :]).then_inc(o_stored[half], 16)

            load_v(Group(0, 0))
            place_m(Group(0, 0))

            def step(g, last):
                if not last:
                    if g.first:
                        sp.wait_ge(rows_ready, 3 * len(more))
                    else:
                        sp.wait_ge(s_tile, g.at(TILES))
                    load(g.next(2))
                    sp.wait_ge(vx_ready, g.at(1, 1))
                    load_v(g.next(1))
                if last:
                    for half in range(2):
                        sp.wait_ge(o_stored[half], 16 * (NG - GPB))
                    sp.dma_start(den[:], scratch["o_rows"][0:EARLY, D].rearrange("r f n -> r (f n)")).then_inc(den_loaded, 16)
                    chunk.load_num(sp, scratch, 0)
                    chunk.load_x1(sp, scratch, 0)
                if not g.first:
                    store(g.next(-1), 1)
                if last:
                    sp.wait_ge(r_ready, 1)
                    sp.dma_start(scratch["r"][0:EARLY, :], den[:]).then_inc(r_stored, 16)
                else:
                    place_m(g.next(1))
                store(g, 0)

            groups(sp, step)
            sp.wait_ge(r_stored, 16)
            chunk.load_rden(sp, scratch, 0)
            store(Group(0, NG - 1), 1)
            for half in range(2):
                sp.wait_ge(o_stored[half], 16 * NG)

        @block.gpsimd
        def _(pool):
            ones, rows = Chain(pool, ones_ready, 0), Chain(pool, rows_ready, 0)
            for n in range(NBUF):
                ones(pool.memset(vx[n][:], 1.0))
            for n in more:
                ahead.rows(rows, pool, qs[n], ks[n])

            def expand_v(g):
                pool.wait_ge(v_loaded, g.at(16, 16))
                hold.pool(pool, ND, zero)
                pool.tensor_copy(vx[g.buf][:, :, :, 0:D],
                                 vin[:].rearrange("p k (h d) -> p k h d", h=GH)).then_inc(vx_ready, 1)

            def step(g, last):
                for s in DIAG_SLOTS:
                    pool.wait_ge(p_ready, g.at(TILES, GH * (s + 1)))
                    hold.pool(pool, DIAG_SLOTS.index(s), zero)
                    for n, off in enumerate(DIAG[s]):
                        blk = probs[:, s % NBUF, :, off:off + P]
                        ins = pool.affine_select(out=blk, in_=blk, compare_op=ALU.is_ge, fill=0.0, base=0,
                                                 pattern=[[0, GH], [1, P]], channel_multiplier=-1)
                    ins.then_inc(p_masked, 1)
                    if s == LOW_DONE and not last:
                        expand_v(g.next(1))

            expand_v(Group(0, 0))
            groups(pool, step)

        @block.scalar
        def _(act):
            def out_m(g):
                act.wait_ge(m_turned, g.at(1, 1))
                if not g.first:
                    p = g.next(-1)
                    act.wait_ge(m_placed[p.buf], p.turn(16, 16))
                act.copy(mt[:], m_bank[M_BANK][0:2 * GH * KT, 0:P]).then_inc(m_out, 1)

            def out_o(g, half):
                act.wait_ge(pv_done, g.at(NSLOT, (LOW_DONE, HIGH_DONE)[half] + 1))
                if not g.first:
                    act.wait_ge(o_stored[half], g.at(16))
                act.copy(o[:, half, :], o_bank[half][:]).then_inc(o_out, 1)

            def exp(g, s, last):
                if not (g.first and s < NBUF):
                    act.wait_ge(pv_done, g.at(NSLOT, s - NBUF + 1))
                for h in range(GH):
                    t = s * GH + h
                    act.wait_ge(s_tile, g.at(TILES, t + 1))
                    act.activation(probs[:, s % NBUF, h, :], score_bank(t, last)[:], ACT.Exp).then_inc(p_ready, 1)

            def step(g, last):
                for s in range(NSLOT):
                    exp(g, s, last)
                    if s == 2 and not g.first:
                        out_o(g.next(-1), 1)
                    if s == NSLOT - AHEAD and not last:
                        out_m(g.next(1))
                    if s == LOW_DONE + 3:
                        out_o(g, 0)

            out_m(Group(0, 0))
            groups(act, step)
            out_o(Group(0, NG - 1), 1)

        @block.vector
        def _(dve):
            dve.memset(mparts[:].bitcast(F32), 0.0).then_inc(z_ready, 1)
            dve.wait_ge(z_ready, 1)

            def maximum(g, a, h):
                t = a * GH + h
                bank = m_bank[t % SB]
                pieces = [(i, bank[:, off:off + n], n, off, k0 + n == (i + 1) * P) for i, k0, n, off in MAX_SLOTS[a]]
                dve.wait_ge(m_tile, g.at(TILES, t + 1))
                if any(diagonal for *_, diagonal in pieces):
                    if not (g.first and t < SB):
                        dve.wait_ge(m_read, g.at(TILES, t - SB + 1))
                    hold.dve(dve, t % 4)
                for i, src, n, off, diagonal in pieces:
                    if diagonal:
                        ins = dve.tensor_tensor_reduce(junk[:, t % SB, off:off + n], src, mask[:, BANK - n:BANK], 1.0, 0.0, ALU.add,
                                                       ALU.max, pm[:, g.buf, 0, h, i:i + 1])
                    else:
                        ins = dve.tensor_reduce(pm[:, g.buf, 1, h, i:i + 1], src, AX.X, ALU.max)
                ins.then_inc(m_read, 1)

            def part(g, n):
                if n == 0:
                    dve.wait_ge(m_read, g.at(TILES, TILES))
                    two = slice(KT // 2, KT)
                    dve.tensor_tensor(pm[:, g.buf, 0, :, two], pm[:, g.buf, 0, :, two], pm[:, g.buf, 1, :, two],
                                      ALU.max).then_inc(m_chain, 1)
                    return
                if n == 1 and not g.first:
                    dve.wait_ge(m_turned, g.at(1))
                dve.wait_ge(m_chain, g.at(3, n))
                whole = pm[:, g.buf, 0, :, :].rearrange("p h i -> p (h i)")
                if n == 1:
                    ins = dve.tensor_scalar(mparts[:, 0, :], whole, -1.0, None, ALU.mult)
                else:
                    ins = dve.scalar_tensor_tensor(out=mparts[:, 1, :], in0=whole, scalar=-1.0,
                                                   in1=mparts[:, 0, :].bitcast(F32), op0=ALU.mult, op1=ALU.subtract)
                ins.then_inc(m_chain, 1)

            def next_maxima(g):
                for a in range(AHEAD):
                    for h in range(GH):
                        if a == 0 and h < 3:
                            part(g, h)
                        maximum(g.next(1), a, h)

            def step(g, last):
                if last:
                    dve.wait_ge(den_loaded, 16)
                    dve.reciprocal(den[:], den[:]).then_inc(r_ready, 1)
                    dve.wait_ge(chunk.o_loaded, chunk.LOADS)
                    for ch in range(KC):
                        dve.tensor_tensor(chunk.on[:, ch, :], chunk.num[:, ch, :], chunk.rden[:, ch, :],
                                          ALU.mult).then_inc(chunk.on_ready, 1)
                    return
                for a in range(AHEAD, NSLOT):
                    for h in range(GH):
                        maximum(g.next(1), a, h)
                next_maxima(g.next(1))

            for a in range(NSLOT):
                for h in range(GH):
                    maximum(Group(0, 0), a, h)
            next_maxima(Group(0, 0))
            groups(dve, step)

        @block.tensor
        def _(pe):
            def turn_m(g):
                pe.wait_ge(m_chain, g.at(3, 3))
                pe.wait_ge(m_read, g.at(TILES, TILES + M_BANK + 1))
                pe.transpose(m_bank[M_BANK][:, 0:P],
                             mparts[:].rearrange("p q n -> p (q n)").bitcast(F32), ident[:]).then_inc(m_turned, 1)

            def max_tile(g, a, h):
                t = a * GH + h
                if t == 0:
                    pe.wait_ge(stacked[g.buf], g.turn(STACK, STACK))
                if not (g.first and t < SB):
                    pe.wait_ge(m_read, g.at(TILES, t - SB + 1))
                if t == TURN_NEXT and not g.first:
                    pe.wait_ge(m_out, g.at(1))
                for i, k0, n, off in MAX_SLOTS[a]:
                    last = pe.matmul(m_bank[t % SB][:, off:off + n], qs[g.buf][0:SROWS, h, i * P:(i + 1) * P],
                                     ks[g.buf][0:SROWS, h, k0:k0 + n], start=True, stop=True)
                last.then_inc(m_tile, 1)

            def score_tile(g, s, h, last):
                t = s * GH + h
                if t == 0:
                    pe.wait_ge(m_placed[g.buf], g.turn(16, 16))
                if last and t == SB:
                    pe.wait_ge(m_read, NG * TILES + AHEAD * GH)
                elif last and t > SB:
                    if t >= 2 * SB:
                        pe.wait_ge(p_ready, g.at(TILES, t - 2 * SB + 1))
                elif not (g.first and t < SB):
                    pe.wait_ge(p_ready, g.at(TILES, t - SB + 1))
                for j, q0, n, off in SLOTS[s]:
                    done = pe.matmul(score_bank(t, last)[:, off:off + n], ks[g.buf][:, h, j * P:(j + 1) * P],
                                     qs[g.buf][:, h, q0:q0 + n], start=True, stop=True)
                done.then_inc(s_tile, 1)

            def values(g, s):
                pe.wait_ge(p_ready, g.at(TILES, GH * (s + 1)))
                if DIAG[s]:
                    pe.wait_ge(p_masked, g.at(ND, DIAG_SLOTS.index(s) + 1))
                if s == 0:
                    pe.wait_ge(vx_ready, g.at(1, 1))
                if s < 2 and not g.first:
                    pe.wait_ge(o_out, g.at(2, s - 1))
                for j, q0, n, off in SLOTS[s]:
                    half, col = q0 // BANK, q0 % BANK
                    for h in range(GH):
                        last = pe.matmul(o_bank[half][2 * D * h:2 * D * (h + 1), col:col + n], vx[g.buf][:, j, h, :],
                                         probs[:, s % NBUF, h, off:off + n], start=(j == 0),
                                         stop=(s in (LOW_DONE, HIGH_DONE) and half == (s == HIGH_DONE)),
                                         tile_position=(0, 2 * D * h))
                last.then_inc(pv_done, 1)

            def step(g, last):
                for s in range(NSLOT):
                    for h in range(GH):
                        score_tile(g, s, h, last)
                        if s == NSLOT - AHEAD + 1 and h == 0 and not last:
                            turn_m(g.next(1))
                        if not last:
                            a = s + AHEAD
                            if a < NSLOT:
                                max_tile(g.next(1), a, h)
                            else:
                                max_tile(g.next(2), a - NSLOT, h)
                    if s >= 2:
                        values(g, s - 2)
                    elif not g.first:
                        values(g.next(-1), NSLOT - 2 + s)

            for a in range(NSLOT):
                for h in range(GH):
                    max_tile(Group(0, 0), a, h)
            for a in range(AHEAD):
                for h in range(GH):
                    max_tile(Group(0, 1), a, h)
                if a == 0:
                    turn_m(Group(0, 0))
            pe.wait_ge(rows_ready, 3 * len(more))
            groups(pe, step)
            for s in (NSLOT - 2, NSLOT - 1):
                values(Group(0, NG - 1), s)


def stage_c(nc, psum, const, io, scratch, chunk):
    ident, mhalf, zero, hbias, wh, wl, hold = const
    with ExitStack() as ctx:
        ar = Arena(nc, ctx, hold)
        banks = {"T": psum[0:2], "F": [psum[2:4], psum[4:6]]}
        o_bank = psum[6:8]
        num, rden, on, x1, LOADS = chunk.num, chunk.rden, chunk.on, chunk.x1, chunk.LOADS
        o_loaded, x1_loaded, on_ready = chunk.o_loaded, chunk.x1_loaded, chunk.on_ready
        oh = ar.sb("c_oh", [P, KC, CHUNK], F32R)
        ol = ar.sb("c_ol", [P, KC, CHUNK], F32R)
        den = ar.sb("c_den", [P, T * H // P])
        x2 = ar.sb("c_x2", [P, TPC, E])
        out = ar.sb("c_out", [P, TPC, E])
        ln = Norm(ar, "c_ln", banks, zero)
        ffn = Experts(ar, "c_ffn", (wh, wl), banks, ln)
        den_loaded = ar.sem("c_den_loaded")
        r_ready = ar.sem("c_r_ready")
        r_stored = ar.sem("c_r_stored")
        oh_ready = ar.sem("c_oh_ready")
        ol_ready = ar.sem("c_ol_ready")
        op_ready = ar.sem("c_op_ready")
        x2_ready = ar.sem("c_x2_ready")
        stored = ar.sem("c_stored")
        c_ready = ar.sem("c_c_ready")

        block = ctx.enter_context(nc.Block())

        @block.sync
        def _(sp):
            def load_o(c):
                chunk.load_num(sp, scratch, c)
                chunk.load_rden(sp, scratch, c)

            def store(c):
                sp.wait_ge(ffn.out_ready, c * TPC + TPC)
                sp.dma_start(io["out"][bass.ds(c, 1)].rearrange("a p t e -> p (a t) e"), out[:]).then_inc(stored, 16)

            def step(c, prev2, nxt, nxt2):
                if nxt:
                    sp.wait_ge(x2_ready, c * TPC + TPC)
                    chunk.load_x1(sp, scratch, c + 1)
                if nxt2:
                    sp.wait_ge(on_ready, c * KC + 2 * KC)
                    load_o(c + 2)
                if prev2:
                    store(c - 2)

            sp.dma_start(den[:], scratch["o_rows"][EARLY:B * H, D].rearrange("h f (q n) -> h (f q) n", n=T * H // P)).then_inc(den_loaded, 16)
            sp.wait_ge(on_ready, KC)
            load_o(1)
            step(0, False, True, True)
            sp.wait_ge(r_ready, 1)
            sp.dma_start(scratch["r"][EARLY:B * H, :].rearrange("h (q n) -> (h q) n", n=T * H // P), den[:]).then_inc(r_stored, 16)
            sp.wait_ge(r_stored, 16)
            step(1, False, True, True)
            with loop(sp, 2, NCHUNK - 2) as c:
                step(c, True, True, True)
            step(NCHUNK - 2, True, True, False)
            step(NCHUNK - 1, True, False, False)
            store(NCHUNK - 2)
            store(NCHUNK - 1)
            sp.wait_ge(stored, NCHUNK * 16)

        @block.gpsimd
        def _(pool):
            pool.memset(ffn.ex[:], 0.0).then_inc(c_ready, 1)

            def divide(c):
                pool.wait_ge(o_loaded, c * LOADS + LOADS)
                pool.wait_ge(ol_ready, c * KC)
                for ch in range(KC):
                    pool.tensor_tensor(on[:, ch, :], num[:, ch, :], rden[:, ch, :], ALU.mult).then_inc(on_ready, 1)

            def low(c):
                for ch in range(KC):
                    pool.wait_ge(oh_ready, c * KC + ch + 1)
                    pool.tensor_tensor(ol[:, ch, :], on[:, ch, :], oh[:, ch, :].bitcast(F32),
                                       ALU.subtract).then_inc(ol_ready, 1)

            def step(c, nxt, first=False):
                if nxt:
                    divide(c + 1)
                    low(c + 1)
                ln.pool_rstd(pool, c, mhalf, first)
                ffn.pool_xb(pool, c, x2, hbias, first)

            step(0, True, True)
            with loop(pool, 1, NCHUNK - 1) as c:
                step(c, True)
            step(NCHUNK - 1, False)

        @block.scalar
        def _(act):
            act.wait_ge(c_ready, 1)

            def high(c, first=False):
                if not first:
                    act.wait_ge(op_ready, c * TPC)
                for ch in range(KC):
                    act.wait_ge(on_ready, c * KC + ch + 1)
                    act.copy(oh[:, ch, :], on[:, ch, :]).then_inc(oh_ready, 1)

            def step(c, prev, here, nxt, prev_first=False):
                k = FIRST if prev_first else c - 1

                def normalise(*tiles):
                    if here:
                        ln.act_normalise(act, c, x2, not prev, tiles)

                if prev:
                    ln.act_high(act, k)
                if nxt:
                    high(c + 1)
                if prev:
                    ffn.act_tile(act, k, 0, prev_first)
                    ffn.act_tile(act, k, 1, prev_first)
                normalise(0, 1)
                if prev:
                    ffn.act_tile(act, k, 2, prev_first)
                normalise(2, 3)
                if prev:
                    ffn.act_tile(act, k, 3, prev_first)
                if prev:
                    ffn.act_exp(act, k)

            high(0, True)
            step(0, False, True, True)
            step(1, True, True, True, True)
            with loop(act, 2, NCHUNK - 1) as c:
                step(c, True, True, True)
            step(NCHUNK - 1, True, True, False)
            step(NCHUNK, True, False, False)

        @block.vector
        def _(dve):
            def output(c, t):
                if t == 0:
                    if not (isinstance(c, int) and c == 0):
                        dve.wait_ge(stored, c * 16)
                ffn.dve_out(dve, c, t, out)

            def residual(c, tiles, later=True):
                for t in tiles:
                    if t == 0:
                        dve.wait_ge(x1_loaded, c * 16 + 16)
                    if later:
                        dve.wait_ge(ln.xn_ready, c * TPC - TPC + t + 1)
                        dve.wait_ge(ffn.xb_ready, c * TPC - TPC + t + 1)
                    dve.wait_ge(op_ready, c * TPC + t + 1)
                    dve.tensor_tensor(x2[:, t, :], o_bank[t % 2][:, (t // 2) * E:(t // 2 + 1) * E], x1[:, t, :],
                                      ALU.add).then_inc(x2_ready, 1)

            def stats(c, tiles):
                for t in tiles:
                    dve.wait_ge(x2_ready, c * TPC + t + 1)
                    ln.dve_stats(dve, c, t, x2)

            def step(c, prev2, prev, here):
                def collect(t):
                    if prev2:
                        dve.wait_ge(ffn.out_ready, c * TPC - 2 * TPC + t + 1)
                    ffn.dve_tile(dve, c - 1, t)

                if here:
                    residual(c, (0,), prev)
                if here:
                    residual(c, (1,), prev)
                if prev2:
                    ffn.dve_gate(dve, c - 2)
                if prev:
                    ln.dve_low(dve, c - 1, (0,))
                if prev:
                    ln.dve_low(dve, c - 1, (1,))
                if here:
                    residual(c, (2,), prev)
                if here:
                    residual(c, (3,), prev)
                if here:
                    stats(c, (0,))
                if here:
                    stats(c, (1,))
                if here:
                    stats(c, (2,))
                if here:
                    stats(c, (3,))
                if here:
                    ln.dve_aggregate(dve, c, not prev)
                if prev2:
                    output(c - 2, 0)
                if prev:
                    collect(0)
                if prev2:
                    output(c - 2, 1)
                if prev2:
                    output(c - 2, 2)
                if prev:
                    collect(1)
                if prev2:
                    output(c - 2, 3)
                if prev:
                    collect(2)
                if prev:
                    collect(3)
                if prev:
                    ffn.dve_logits(dve, c - 1)

            for ch in range(KC):
                dve.wait_ge(oh_ready, ch + 1)
                dve.tensor_tensor(ol[:, ch, :], on[:, ch, :], oh[:, ch, :].bitcast(F32), ALU.subtract).then_inc(ol_ready, 1)
            step(0, False, False, True)
            dve.wait_ge(den_loaded, 16)
            dve.reciprocal(den[:], den[:]).then_inc(r_ready, 1)
            step(1, False, True, True)
            step(2, True, True, True)
            with loop(dve, 3, NCHUNK) as c:
                step(c, True, True, True)
            step(NCHUNK, True, True, False)
            step(NCHUNK + 1, True, False, False)

        @block.tensor
        def _(pe):
            def project_out(c, later, tiles):
                if tiles[0] == 0:
                    pe.wait_ge(ol_ready, c * KC + KC)
                    if later:
                        pe.wait_ge(x2_ready, c * TPC)
                cols = slice(W_OUT, W_OUT + E)
                for t in tiles:
                    if t >= 2:
                        pe.wait_ge(x2_ready, c * TPC + t - 1)
                    toks = slice(t * P, (t + 1) * P)
                    project(pe, o_bank[t % 2][:, (t // 2) * E:(t // 2 + 1) * E],
                            [oh[:, ch, toks] for ch in range(KC)], [ol[:, ch, toks] for ch in range(KC)],
                            [wh[:, ch, cols] for ch in range(KC)],
                            [wl[:, ch, cols] for ch in range(KC)]).then_inc(op_ready, 1)

            def step(c, prev, here=True, prev_first=False):
                k = FIRST if prev_first else c - 1
                if here:
                    project_out(c, prev, range(2))
                if prev:
                    ln.pe_transpose(pe, k, ident)
                if here:
                    project_out(c, prev, range(2, TPC))
                if prev:
                    for t in range(TPC):
                        ffn.pe_tile(pe, k, t)

            step(0, False)
            step(1, True, prev_first=True)
            pairs(pe, 2, NCHUNK, lambda c: step(c, True))
            step(NCHUNK, True, here=False)


def macaron(nc, x, wqkv_t, wsh_t, wex_t, wgate, wout_t, bias, out):
    scr_qk = nc.dram_tensor("scr_qk", [B, 2, 2, E, T // CHUNK, CHUNK], F32).ap()
    scr_v = nc.dram_tensor("scr_v", [NCHUNK, TPC, P, E], F32).ap()
    scr_x1 = nc.dram_tensor("scr_x1", [NCHUNK, P, TPC, E], F32).ap()
    scr_o = nc.dram_tensor("scr_o", [NG, P, 2, CHUNK], F32).ap()
    scr_r = nc.dram_tensor("scr_r", [B * H, T], F32).ap()
    scratch = {
        "qk": scr_qk,
        "qk_b": scr_qk.rearrange("b k q (g h d) f n -> b k q g h d (f n)", g=GPB, h=GH),
        "v": scr_v,
        "v_b": scr_v.rearrange("(b f) t p (g n) -> b (f t) p g n", f=2, g=GPB),
        "x1": scr_x1,
        "o": scr_o,
        "o_rows": scr_o.rearrange("g (h r) f n -> (g h) r f n", h=GH),
        "r": scr_r,
    }
    io = {
        "x": x.rearrange("(c t p) e -> c p t e", t=TPC, p=P),
        "out": out.rearrange("(c t p) e -> c p t e", t=TPC, p=P),
        "weights": {"qkv": (wqkv_t, W_QK), "shared": (wsh_t, W_SH), "expert": (wex_t, W_EX), "gate": (wgate, W_EX + E),
                    "out": (wout_t, W_OUT)},
        "bias": bias,
    }
    with ExitStack() as ctx:
        ar = Arena(nc, ctx)
        psum = [ctx.enter_context(nc.psum_tensor(f"bank{n}", [P, BANK], F32)) for n in range(8)]
        ident = ar.sb("ident", [P, P])
        mhalf = ar.sb("mhalf", [P, TPC])
        zero = ar.sb("zero", [P, TPC])
        hbias = ar.sb("hbias", [P, E])
        wh = ar.sb("wh", [P, KC, WCOLS], F32R)
        wl = ar.sb("wl", [P, KC, WCOLS], F32R)
        const = (ident, mhalf, zero, hbias, wh, wl, Hold(ar))
        chunk = Attended(ar)
        with ExitStack() as both:
            ahead = Ahead(Arena(nc, both))
            stage_a(nc, psum, const, io, scratch, ahead)
            stage_b(nc, psum, const, scratch, ahead, chunk)
        stage_c(nc, psum, const, io, scratch, chunk)


def kernel(**inputs):
    import numpy as np
    import concourse.bacc as bacc
    from concourse.bass_utils import run_bass_kernel_spmd

    x = np.asarray(inputs["L0_attn_query"])
    arrays = {
        "x": np.ascontiguousarray(x.reshape(B * T, E)),
        "wqkv_t": np.ascontiguousarray(np.asarray(inputs["L0_attn_in_proj_weight"]).T),
        "wsh_t": np.ascontiguousarray(np.asarray(inputs["L0_ffn_W_shared"]).T),
        "wex_t": np.ascontiguousarray(np.asarray(inputs["L0_ffn_W_expert"]).T),
        "wgate": np.ascontiguousarray(np.asarray(inputs["L0_ffn_W_gate"])),
        "wout_t": np.ascontiguousarray(np.asarray(inputs["L0_attn_out_proj_weight"]).T),
        "bias": np.ascontiguousarray(np.asarray(inputs["L0_ffn_bias"])),
    }
    nc = bacc.Bacc("TRN2", target_bir_lowering=False, num_devices=1)
    nc.disable_value_cache = True
    args = [nc.dram_tensor(n, a.shape, mybir.dt.from_np(a.dtype), kind="ExternalInput").ap() for n, a in arrays.items()]
    out = nc.dram_tensor("out", [B * T, E], F32, kind="ExternalOutput").ap()
    macaron(nc, *args, out)
    got = run_bass_kernel_spmd(nc, [arrays], core_ids=[0])
    return got.results[0]["out"].reshape(B, T, E)
```
